# Optimizing a Trainium2 kernel written in Bass

```python
import numpy as np
import jax
import jax.numpy as jnp

def _softmax(x, axis=-1):
    return jax.nn.softmax(x, axis=axis)

def _gelu(x):
    return jax.nn.gelu(x, approximate=True)

def _silu(x):
    return jax.nn.silu(x)

def _sigmoid(x):
    return jax.nn.sigmoid(x)

def _layernorm(x, axis=-1, eps=1e-05):
    m = jnp.mean(x, axis=axis, keepdims=True)
    v = jnp.var(x, axis=axis, keepdims=True)
    return (x - m) / jnp.sqrt(v + eps)

def _scatter_add(tgt, idx, src, axis=0):
    return tgt.at[idx].add(src)

def _segment_sum(src, seg, n):
    return jax.ops.segment_sum(src, seg, n)
kernel_name = 'mk_seq_postln_d1_jaxref_r8_f17f9a'

def setup_inputs(seed: int=0):
    np.random.seed(seed)
    _w = jnp.asarray

    def _L0_attn_setup():
        import jax, jax.numpy as jnp
        import numpy as np
        H, KV, HD, HID = (32, 8, 128, 512)
        THETA, FACTOR, HI_FF, LO_FF, ORIG_MAX = (500000.0, 8.0, 4.0, 1.0, 1024)

        def _llama3_inv_freq():
            inv = 1.0 / THETA ** (np.arange(0, HD, 2, dtype=np.float64) / HD)
            wavelen = 2.0 * np.pi / inv
            low_wl = ORIG_MAX / LO_FF
            high_wl = ORIG_MAX / HI_FF
            smooth = (ORIG_MAX / wavelen - LO_FF) / (HI_FF - LO_FF)
            scaled = np.where(wavelen > low_wl, inv / FACTOR, inv)
            mid = (wavelen <= low_wl) & (wavelen >= high_wl)
            scaled = np.where(mid, (1 - smooth) * inv / FACTOR + smooth * inv, scaled)
            return scaled.astype(np.float32)

        def _rope_cos_sin(T):
            inv = _llama3_inv_freq()
            pos = np.arange(T, dtype=np.float32)
            freqs = pos[:, None] * inv[None, :]
            emb = np.concatenate([freqs, freqs], axis=-1)
            return (jnp.asarray(np.cos(emb)), jnp.asarray(np.sin(emb)))

        def _rotate_half(x):
            x1, x2 = jnp.split(x, 2, axis=-1)
            return jnp.concatenate([-x2, x1], axis=-1)
        key = jax.random.key(seed)
        ks = jax.random.split(key, 5)
        s = 1.0 / np.sqrt(HID)
        return {'x': jax.random.normal(ks[0], (1, 256, HID), jnp.float32), 'wq': jax.random.normal(ks[1], (HID, H * HD), jnp.float32) * s, 'wk': jax.random.normal(ks[2], (HID, KV * HD), jnp.float32) * s, 'wv': jax.random.normal(ks[3], (HID, KV * HD), jnp.float32) * s, 'wo': jax.random.normal(ks[4], (H * HD, HID), jnp.float32) * s}
    _L0_attn_in = _L0_attn_setup()

    def _L0_ffn_setup():
        import jax, jax.numpy as jnp
        import numpy as np
        RMS_EPS = 1e-05
        key = jax.random.key(seed)
        k1, k2, k3, k4 = jax.random.split(key, 4)
        B, S, H, I = (1, 256, 512, 1792)
        x = jax.random.normal(k1, (B, S, H), dtype=jnp.float32)
        ln_w = jnp.ones((H,), dtype=jnp.float32)
        gate_w = jax.random.normal(k2, (I, H), dtype=jnp.float32) * 0.02
        up_w = jax.random.normal(k3, (I, H), dtype=jnp.float32) * 0.02
        down_w = jax.random.normal(k4, (H, I), dtype=jnp.float32) * 0.02
        return {'x': x, 'ln_w': ln_w, 'gate_w': gate_w, 'up_w': up_w, 'down_w': down_w}
    _L0_ffn_in = _L0_ffn_setup()
    _d = {'L0_attn_x': _L0_attn_in['x'], 'L0_attn_wq': _L0_attn_in['wq'], 'L0_attn_wk': _L0_attn_in['wk'], 'L0_attn_wv': _L0_attn_in['wv'], 'L0_attn_wo': _L0_attn_in['wo'], 'L0_ffn_ln_w': _L0_ffn_in['ln_w'], 'L0_ffn_gate_w': _L0_ffn_in['gate_w'], 'L0_ffn_up_w': _L0_ffn_in['up_w'], 'L0_ffn_down_w': _L0_ffn_in['down_w']}
    _x0 = _d['L0_attn_x']
    _d['L0_attn_x'] = jax.random.normal(jax.random.fold_in(jax.random.key(seed), 1), (1, 1024, 512), dtype=_x0.dtype)
    del _x0
    return _d

def reference(L0_attn_x, L0_attn_wq, L0_attn_wk, L0_attn_wv, L0_attn_wo, L0_ffn_ln_w, L0_ffn_gate_w, L0_ffn_up_w, L0_ffn_down_w):

    def _L0_attn_ref(x, wq, wk, wv, wo):
        import jax, jax.numpy as jnp
        import numpy as np
        H, KV, HD, HID = (32, 8, 128, 512)
        THETA, FACTOR, HI_FF, LO_FF, ORIG_MAX = (500000.0, 8.0, 4.0, 1.0, 1024)

        def _llama3_inv_freq():
            inv = 1.0 / THETA ** (np.arange(0, HD, 2, dtype=np.float64) / HD)
            wavelen = 2.0 * np.pi / inv
            low_wl = ORIG_MAX / LO_FF
            high_wl = ORIG_MAX / HI_FF
            smooth = (ORIG_MAX / wavelen - LO_FF) / (HI_FF - LO_FF)
            scaled = np.where(wavelen > low_wl, inv / FACTOR, inv)
            mid = (wavelen <= low_wl) & (wavelen >= high_wl)
            scaled = np.where(mid, (1 - smooth) * inv / FACTOR + smooth * inv, scaled)
            return scaled.astype(np.float32)

        def _rope_cos_sin(T):
            inv = _llama3_inv_freq()
            pos = np.arange(T, dtype=np.float32)
            freqs = pos[:, None] * inv[None, :]
            emb = np.concatenate([freqs, freqs], axis=-1)
            return (jnp.asarray(np.cos(emb)), jnp.asarray(np.sin(emb)))

        def _rotate_half(x):
            x1, x2 = jnp.split(x, 2, axis=-1)
            return jnp.concatenate([-x2, x1], axis=-1)
        B, T, _ = x.shape
        q = (x @ wq).reshape(B, T, H, HD).transpose(0, 2, 1, 3)
        k = (x @ wk).reshape(B, T, KV, HD).transpose(0, 2, 1, 3)
        v = (x @ wv).reshape(B, T, KV, HD).transpose(0, 2, 1, 3)
        cos, sin = _rope_cos_sin(T)
        q = q * cos + _rotate_half(q) * sin
        k = k * cos + _rotate_half(k) * sin
        rep = H // KV
        k = jnp.repeat(k, rep, axis=1)
        v = jnp.repeat(v, rep, axis=1)
        scores = jnp.einsum('bhtd,bhsd->bhts', q, k) * (1.0 / np.sqrt(HD))
        mask = jnp.tril(jnp.ones((T, T), dtype=bool))
        scores = jnp.where(mask, scores, -jnp.inf)
        att = jax.nn.softmax(scores, axis=-1)
        out = jnp.einsum('bhts,bhsd->bhtd', att, v)
        out = out.transpose(0, 2, 1, 3).reshape(B, T, H * HD)
        return out @ wo

    def _L0_ffn_ref(x, ln_w, gate_w, up_w, down_w):
        import jax, jax.numpy as jnp
        import numpy as np
        RMS_EPS = 1e-05
        var = jnp.mean(jnp.square(x), axis=-1, keepdims=True)
        nx = x * jax.lax.rsqrt(var + RMS_EPS) * ln_w
        g = jnp.einsum('bsh,ih->bsi', nx, gate_w)
        u = jnp.einsum('bsh,ih->bsi', nx, up_w)
        return jnp.einsum('bsi,hi->bsh', jax.nn.silu(g) * u, down_w)
    x = L0_attn_x
    x = _layernorm(x + _L0_attn_ref(x, L0_attn_wq, L0_attn_wk, L0_attn_wv, L0_attn_wo), axis=-1)
    x = _layernorm(x + _L0_ffn_ref(x, L0_ffn_ln_w, L0_ffn_gate_w, L0_ffn_up_w, L0_ffn_down_w), axis=-1)
    return x

_drawn_inputs = setup_inputs


def setup_inputs(seed=0):
    import zlib

    import numpy as np

    out = dict(_drawn_inputs(seed))
    spreads = {'L0_ffn_ln_w': (1.0, 0.2)}
    factors = {}
    for name, (base, spread) in spreads.items():
        noise = np.random.default_rng([zlib.crc32(name.encode()), seed]).standard_normal(out[name].shape)
        drawn = base * np.exp(spread * noise) if base else spread * noise
        out[name] = jnp.asarray(drawn.astype(out[name].dtype))
    for name, factor in factors.items():
        out[name] = (out[name] * factor).astype(out[name].dtype)
    return out
```

```python
from contextlib import ExitStack

import concourse.bass as bass
from concourse import mybir

F32 = mybir.dt.float32
F32R = mybir.dt.float32r
BF16 = mybir.dt.bfloat16
ALU = mybir.AluOpType
ACT = mybir.ActivationFunctionType
AX = mybir.AxisListType

P = 128
HEADS, KV_HEADS, HD = 32, 8, 128
T, HID, INTER = 1024, 512, 1792
REP = HEADS // KV_HEADS
NT = T // P
NC = HID // P
HALF = T // 2
HT = NT // 2
GROUPS = KV_HEADS
PAIRS = INTER // (2 * P)
LN_EPS = 1e-5
RMS_EPS = 1e-5
MASKED = -3.0e38


class Tally:

    PER = {
        "tile": REP * NT,
        "pt": REP * 12,
        "unit": REP * 13 + 2,
        "rope": REP * 2 + 2,
        "ohi": REP * 2 + 2,
        "recip": REP * 2,
        "wq": REP, "wo": REP, "wkv": 2,
        "stats": 0,
    }

    def __init__(self):
        self.n = dict.fromkeys(self.PER, 0)
        self.group = 0

    def __getitem__(self, kind):
        return self.n[kind] + self.PER[kind] * self.group

    def at(self, kind, local):
        return local + self.PER[kind] * self.group

    def add(self, kind, count=1):
        self.n[kind] += count

    def enter(self, group):
        self.group = group

    def leave(self, iterations):
        self.group = 0
        for kind, per in self.PER.items():
            self.n[kind] += per * (iterations - 1)


def extras(j, i, first=False, last=False):
    if i == 0:
        return [] if first else [("y", 2), ("y", 3)]
    if i == 1:
        return [] if first else [("pv", 1)]
    if i == 2:
        ys = [] if first else [("y", t) for t in range(HT, NT)]
        return ys + ([("vt", 0), ("vt", 1)] if j % REP == 0 else [])
    if i in (3, 4):
        return [] if last and j == REP - 1 else [("q", i - 3)]
    if i == 5:
        return [("pv", 0)]
    if i == 6:
        return [] if last else [("k", j)] if j < 2 else [("v", j - 2)]
    return [("y", 0), ("y", 1)]


def loop_steps():
    return [divmod(s, NT) for s in range(3, 3 + REP * NT)]


def last_steps():
    return [divmod(s, NT) for s in range(3, REP * NT)]


def tail_steps():
    return [(REP, 0), (REP, 1), (REP, 2)]


def tail_extras(i):
    return [e for e in extras(REP, i) if e[0] != "vt"]


def tp_banks(i):
    return i // 4 + 1


def score_chunks(i):
    width = P * (i + 1)
    if width <= 512:
        return [(0, 0, width)]
    return [(0, 0, width // 2), (512, width // 2, width // 2)]


def layer_kernel(nc, x, wq, wk, wv, wo, ln_w, gate_w, up_w, down_w, cos_t, sin_t, out):
    x_v = x.rearrange("b (i p) d -> p (b i) d", p=P)
    out_v = out.rearrange("b (i p) d -> p (b i) d", p=P)
    wq_v = wq.rearrange("(c p) n -> p c n", p=P)
    wk_v = wk.rearrange("(c p) n -> p c n", p=P)
    wv_v = wv.rearrange("(c p) n -> p c n", p=P)
    ln_w_v = ln_w.rearrange("(c p) -> p c", p=P)
    down_v = down_w.rearrange("(n p) i -> p n i", p=P)

    with ExitStack() as ctx:
        def sb(name, shape, dt=F32):
            return ctx.enter_context(nc.sbuf_tensor(name, [P] + shape, dt))

        def sem(name):
            return ctx.enter_context(nc.semaphore(name))

        y = sb("y", [NT, HID])
        xT_hi, xT_lo = sb("xT_hi", [NC, T], F32R), sb("xT_lo", [NC, T], F32R)
        PT_hi, PT_lo = sb("PT_hi", [12, HALF], F32R), sb("PT_lo", [12, HALF], F32R)
        Q_hi, Q_lo = sb("Q_hi", [2, T], F32R), sb("Q_lo", [2, T], F32R)
        K_hi, K_lo = sb("K_hi", [2, T], F32R), sb("K_lo", [2, T], F32R)
        V_hi, V_lo = sb("V_hi", [NT, HD], F32R), sb("V_lo", [NT, HD], F32R)
        O_hi, O_lo = sb("O_hi", [T], F32R), sb("O_lo", [T], F32R)
        V_stage = sb("V_stage", [T])
        cos_sb, sin_sb = sb("cos_sb", [T]), sb("sin_sb", [T])
        wq_raw, wq_hi, wq_lo = sb("wq_raw", [NC, HD]), sb("wq_hi", [NC, HD], F32R), sb("wq_lo", [NC, HD], F32R)
        wkv_raw, wkv_hi, wkv_lo = sb("wkv_raw", [NC, HD]), sb("wkv_hi", [NC, HD], F32R), sb("wkv_lo", [NC, HD], F32R)
        wo_raw, wo_hi, wo_lo = sb("wo_raw", [HID]), sb("wo_hi", [HID], F32R), sb("wo_lo", [HID], F32R)
        probs = sb("probs", [2, T])
        rope_c, rope_s, rope_sum = sb("rope_c", [2, HALF]), sb("rope_s", [2, HALF]), sb("rope_sum", [2, HALF])
        gate_raw, up_raw = sb("gate_raw", [2, HID]), sb("up_raw", [2, HID])
        ident = sb("ident", [P])
        ident_bf, mask_bf = sb("ident_bf", [P], BF16), sb("mask_bf", [P], BF16)
        neg_max = sb("neg_max", [4])
        row_sum, row_rcp = sb("row_sum", [2, NT]), sb("row_rcp", [2, NT])
        ln_w_sb = sb("ln_w_sb", [NC])
        stats, mean_var, sum_sq = sb("stats", [NT, 6]), sb("mean_var", [NT, 2]), sb("sum_sq", [NT])
        spread, inv_spread = sb("spread", [NT]), sb("inv_spread", [NT])
        zero = sb("zero", [1])
        eps_ln, eps_rms = sb("eps_ln", [1]), sb("eps_rms", [1])

        def part(tensor, at, shape):
            size = shape[0] * shape[1]
            flat = tensor[:].rearrange("p a b -> p (a b)")[:, at:at + size]
            return flat.rearrange("p (a b) -> p a b", b=shape[1])

        gT = [part(t, 0, (NC, 2 * P)) for t in (PT_hi, PT_lo)]
        uT = [part(t, NC * 2 * P, (NC, 2 * P)) for t in (PT_hi, PT_lo)]
        dT = [part(t, NC * 4 * P, (2, HID)) for t in (PT_hi, PT_lo)]
        act = [part(t, NC * 4 * P + 2 * HID, (2, T)) for t in (PT_hi, PT_lo)]
        nx = [b[:, k * HID:(k + 1) * HID] for b in (cos_sb, sin_sb) for k in range(2)]
        nx += [b[:, k] for b in (rope_c, rope_s) for k in range(2)]
        down_raw = part(probs, 0, (NC, 2 * P))

        S = ctx.enter_context(nc.psum_tensor("S", [P, 2, T], F32))
        TP = ctx.enter_context(nc.psum_tensor("TP", [P, 2, HALF], F32))
        ACC = ctx.enter_context(nc.psum_tensor("ACC", [P, 2, HALF], F32))
        xbank = [[S[:, c // 2, (c % 2) * HALF:(c % 2 + 1) * HALF] for c in range(NC)],
                 [TP[:, 0], TP[:, 1], ACC[:, 0], ACC[:, 1]]]

        def pt_views(dst, i, u, bank):
            blocks = min(4, i + 1 - 4 * u)
            row = (0 if i < HT else HT) + 4 * u
            col = (i % HT) * P
            return dst[:, row:row + blocks, col:col + P], TP[:, bank, 0:blocks * P].rearrange("p (a b) -> p a b", b=P)

        x_in, table_in = sem("x_in"), sem("table_in")
        wq_in, wkv_in, wo_in = sem("wq_in"), sem("wkv_in"), sem("wo_in")
        gate_in, up_in, down_in = sem("gate_in"), sem("up_in"), sem("down_in")
        const_done = sem("const_done")
        w_hi_done = sem("w_hi_done")
        wq_done, wkv_done, wo_done = sem("wq_done"), sem("wkv_done"), sem("wo_done")
        xt_done, xt_hi_done, xt_lo_done = sem("xt_done"), sem("xt_hi_done"), sem("xt_lo_done")
        score_done = sem("score_done")
        max_done = sem("max_done")
        exp_done = sem("exp_done")
        tp_done = sem("tp_done")
        tp_hi_done = sem("tp_hi_done")
        tp_lo_done = sem("tp_lo_done")
        unit_done = sem("unit_done")
        unit_free = sem("unit_free")
        unit_hi_done = sem("unit_hi_done")
        rope_sum_done = sem("rope_sum_done")
        rope_hi_done = sem("rope_hi_done")
        rope_lo_done = sem("rope_lo_done")
        rcp_done = sem("rcp_done")
        stats_done = sem("stats_done")
        var_done = sem("var_done")
        std_done = sem("std_done")
        inv_done = sem("inv_done")
        ln_done = sem("ln_done")
        sq_done = sem("sq_done")
        nx_done = sem("nx_done")
        gu_done = sem("gu_done")
        silu_done = sem("silu_done")
        prod_done = sem("prod_done")
        act_hi_done = sem("act_hi_done")
        act_lo_done = sem("act_lo_done")
        out_ready, out_done = sem("out_ready"), sem("out_done")
        eps_done = sem("eps_done")

        block = ctx.enter_context(nc.Block())

        @block.sync
        def _(sp):
            sp.dma_start(y[:], x_v).then_inc(x_in, 16)
            sp.dma_start(wkv_raw[:], wk_v[:, :, 0:HD]).then_inc(wkv_in, 16)
            sp.dma_start(wq_raw[:], wq_v[:, :, 0:HD]).then_inc(wq_in, 16)
            sp.dma_start(cos_sb[:], cos_t).then_inc(table_in, 16)
            sp.dma_start(sin_sb[:], sin_t).then_inc(table_in, 16)
            with nc.allow_non_contiguous_dma(reason="512 words, once"):
                sp.dma_start(ln_w_sb[:], ln_w_v).then_inc(table_in, 16)
            sp.dma_start(wo_raw[:], wo[0:HD, :]).then_inc(wo_in, 16)
            sp.dma_start(gate_raw[:], gate_w[0:2 * P, :].rearrange("(a p) k -> p a k", p=P)).then_inc(gate_in, 16)
            sp.dma_start(up_raw[:], up_w[0:2 * P, :].rearrange("(a p) k -> p a k", p=P)).then_inc(up_in, 16)
            sp.wait_ge(wkv_done, 1)
            sp.dma_start(wkv_raw[:], wv_v[:, :, 0:HD]).then_inc(wkv_in, 16)
            sp.wait_ge(wq_done, 1)
            sp.dma_start(wq_raw[:], wq_v[:, :, HD:2 * HD]).then_inc(wq_in, 16)

            def load_wq(h):
                sp.wait_ge(wq_done, h)
                sp.dma_start(wq_raw[:], wq_v[:, :, bass.ds(h * HD, HD)]).then_inc(wq_in, 16)

            def load_wo(h):
                sp.wait_ge(wo_done, h)
                sp.dma_start(wo_raw[:], wo[bass.ds(h * HD, HD), :]).then_inc(wo_in, 16)

            with sp.Fori(0, GROUPS - 1) as g:
                for j in range(REP):
                    load_wq(g * REP + (j + 2))
                    if j == 0:
                        sp.wait_ge(wkv_done, g * 2 + 2)
                        sp.dma_start(wkv_raw[:], wk_v[:, :, bass.ds(g * HD + HD, HD)]).then_inc(wkv_in, 16)
                    if j == 1:
                        sp.wait_ge(wkv_done, g * 2 + 3)
                        sp.dma_start(wkv_raw[:], wv_v[:, :, bass.ds(g * HD + HD, HD)]).then_inc(wkv_in, 16)
                    load_wo(g * REP + (j + 1))
            for h in range((GROUPS - 1) * REP, HEADS):
                if h + 2 < HEADS:
                    load_wq(h + 2)
                if h + 1 < HEADS:
                    load_wo(h + 1)

            def load_gate_up(p):
                sp.wait_ge(tp_done, tp_base + p * 6 - 2)
                sp.dma_start(gate_raw[:], gate_w[bass.ds(p * 2 * P, 2 * P), :].rearrange("(a p) k -> p a k", p=P)).then_inc(gate_in, 16)
                sp.dma_start(up_raw[:], up_w[bass.ds(p * 2 * P, 2 * P), :].rearrange("(a p) k -> p a k", p=P)).then_inc(up_in, 16)

            def load_down(p):
                sp.dma_start(down_raw, down_v[:, :, bass.ds(p * 2 * P, 2 * P)]).then_inc(down_in, 16)

            tp_base = HEADS * 12
            sp.wait_ge(tp_done, tp_base)
            load_down(0)
            load_gate_up(1)
            with sp.Fori(1, PAIRS - 1) as p:
                sp.wait_ge(tp_done, p * 6 + (tp_base + 4))
                load_down(p)
                load_gate_up(p + 1)
            sp.wait_ge(tp_done, tp_base + (PAIRS - 1) * 6 + 4)
            load_down(PAIRS - 1)

            for t in range(NT):
                sp.wait_ge(out_ready, t + 1)
                sp.dma_start(out_v[:, t, :], y[:, t, :]).then_inc(out_done, 16)
            sp.wait_ge(out_done, 16 * NT)

        @block.gpsimd
        def _(pool):
            n = Tally()

            nc.gpsimd.memset(ident[:], 0.0).then_inc(const_done, 1)
            nc.gpsimd.memset(ident_bf[:], 0.0).then_inc(const_done, 1)
            nc.gpsimd.memset(mask_bf[:], 0.0).then_inc(const_done, 1)
            nc.gpsimd.memset(zero[:], 0.0).then_inc(const_done, 1)
            pool.wait_ge(const_done, 4)
            for m in (ident, ident_bf):
                nc.gpsimd.affine_select(out=m[:], in_=m[:], compare_op=ALU.not_equal, fill=1.0, base=0,
                                        pattern=[[-1, P]], channel_multiplier=1).then_inc(const_done, 1)
            nc.gpsimd.affine_select(out=mask_bf[:], in_=mask_bf[:], compare_op=ALU.is_ge, fill=MASKED, base=0,
                                    pattern=[[-1, P]], channel_multiplier=1).then_inc(const_done, 1)
            def split(kind, raw, hi, lo, arrived, done):
                pool.wait_ge(arrived, n[kind] * 16 + 16)
                nc.gpsimd.tensor_tensor(hi, raw, zero[:, 0:1].to_broadcast([P, NC * HD]), ALU.add).then_inc(w_hi_done, 1)
                pool.wait_ge(w_hi_done, n["wq"] + n["wo"] + n["wkv"] + 1)
                nc.gpsimd.tensor_tensor(lo, raw, hi.bitcast(F32), ALU.subtract).then_inc(done, 1)
                n.add(kind)

            def flat(a):
                return a[:].rearrange("p a b -> p (a b)")

            def split_wq():
                split("wq", flat(wq_raw), flat(wq_hi), flat(wq_lo), wq_in, wq_done)

            def split_wkv():
                split("wkv", flat(wkv_raw), flat(wkv_hi), flat(wkv_lo), wkv_in, wkv_done)

            def split_wo():
                split("wo", wo_raw[:], wo_hi[:], wo_lo[:], wo_in, wo_done)

            def rope_add():
                r = n.n["rope"] % 2
                pool.wait_ge(unit_free, n["unit"] + 1)
                if n.n["rope"] >= 2:
                    pool.wait_ge(rope_lo_done, n["rope"] - 1)
                nc.gpsimd.tensor_tensor(rope_sum[:, r], rope_c[:, r], rope_s[:, r], ALU.add).then_inc(rope_sum_done, 1)
                n.add("rope")

            def rope_low(hi, lo):
                r = (n.n["rope"] - 1) % 2
                pool.wait_ge(rope_hi_done, n["rope"])
                nc.gpsimd.tensor_tensor(lo, rope_sum[:, r], hi.bitcast(F32), ALU.subtract).then_inc(rope_lo_done, 1)

            def half_of(a, slot, half):
                return a[:, slot, half * HALF:(half + 1) * HALF]

            def k_half(a, slot, half):
                return a[:, bass.ds(slot, 1), half * HALF:(half + 1) * HALF].rearrange("p a b -> p (a b)")

            def step(j, i, ex, k_slot, last=False):
                before = n["unit"]
                if i == 1 and not (last and j == REP):
                    pool.wait_ge(unit_done, before)
                    split_wq()
                if i == 3:
                    pool.wait_ge(unit_done, before)
                    split_wo()
                for kind, a in ex:
                    if kind in "qk":
                        rope_add()
                    if kind == "q":
                        rope_low(half_of(Q_hi, (j + 1) % 2, a), half_of(Q_lo, (j + 1) % 2, a))
                    if kind == "k":
                        rope_low(k_half(K_hi, k_slot, a), k_half(K_lo, k_slot, a))
                    n.add("unit")
                if not last and (j, i) in ((0, 5), (1, 7)):
                    pool.wait_ge(unit_done, before)
                    split_wkv()

            split_wkv()
            split_wq()
            for half in range(2):
                rope_add()
                rope_low(half_of(K_hi, 0, half), half_of(K_lo, 0, half))
                n.add("unit")
            pool.wait_ge(unit_done, 2)
            split_wkv()
            n.add("unit", 2)
            for half in range(2):
                rope_add()
                rope_low(half_of(Q_hi, 0, half), half_of(Q_lo, 0, half))
                n.add("unit")
            for i in range(3):
                step(0, i, extras(0, i, first=True), 0)
            with pool.Fori(0, GROUPS - 1) as g:
                n.enter(g)
                k_slot = pool.snap((g + 1) % 2)
                for j, i in loop_steps():
                    step(j, i, extras(j, i), k_slot)
            n.leave(GROUPS - 1)
            for j, i in last_steps():
                if i == 1 and j == REP - 1:
                    for kind, a in extras(j, i, last=True):
                        n.add("unit")
                    continue
                step(j, i, extras(j, i, last=True), 0, last=True)

            def act_low(u, unit_no):
                pool.wait_ge(act_hi_done, unit_no)
                i2, half = divmod(u, 2)
                cols = slice(half * HALF, (half + 1) * HALF)
                nc.gpsimd.tensor_tensor(act[1][:, i2, cols], rope_s[:, u % 2], act[0][:, i2, cols].bitcast(F32),
                                        ALU.subtract).then_inc(act_lo_done, 1)

            with pool.Fori(0, PAIRS) as p:
                for u in range(4):
                    act_low(u, p * 4 + (u + 1))

        @block.scalar
        def _(act_e):
            n = Tally()

            def exponent(j, i):
                slot, at = n.n["tile"] % 2, n.n["tile"] % 4
                act_e.wait_ge(max_done, n["tile"] + 1)
                width = P * (i + 1)
                src, dst = S[:, slot, 0:width], probs[:, slot, 0:width]
                if width > 512:
                    src = S[:, slot].rearrange("p (a b) -> p a b", a=2)[:, :, 0:width // 2]
                    dst = dst.rearrange("p (a b) -> p a b", a=2)
                nc.scalar.activation(dst, src, ACT.Exp, bias=neg_max[:, at:at + 1],
                                     accum_out=row_sum[:, j % 2, i:i + 1]).then_inc(exp_done, 1)
                n.add("tile")

            def tp_high(i):
                for u in range(tp_banks(i)):
                    act_e.wait_ge(tp_done, n["pt"] + 1)
                    dst, src = pt_views(PT_hi, i, u, n.n["pt"] % 2)
                    nc.scalar.activation(dst, src, ACT.Copy).then_inc(tp_hi_done, 1)
                    n.add("pt")

            def rope_high(hi):
                act_e.wait_ge(rope_sum_done, n["rope"] + 1)
                nc.scalar.activation(hi, rope_sum[:, n.n["rope"] % 2], ACT.Copy).then_inc(rope_hi_done, 1)
                n.add("rope")

            def unit_high(dst):
                act_e.wait_ge(unit_done, n["unit"] + 1)
                nc.scalar.activation(dst, ACC[:, n.n["unit"] % 2], ACT.Copy).then_inc(unit_hi_done, 1)

            pending = []

            def flush():
                while pending:
                    rope_high(pending.pop(0))

            def extra_high(j, ex, k_slot):
                for kind, a in ex:
                    if kind == "pv":
                        unit_high(O_hi[:, a * HALF:(a + 1) * HALF])
                    if kind == "vt":
                        unit_high(V_hi[:, a * HT:(a + 1) * HT, :].rearrange("p a b -> p (a b)"))
                    if kind == "q":
                        pending.append(Q_hi[:, (j + 1) % 2, a * HALF:(a + 1) * HALF])
                    if kind == "k":
                        pending.append(K_hi[:, bass.ds(k_slot, 1), a * HALF:(a + 1) * HALF].rearrange("p a b -> p (a b)"))
                    n.add("unit")

            def step(j, i, ex, k_slot, more=True):
                if more:
                    exponent(j + (i + 1) // NT, (i + 1) % NT)
                flush()
                extra_high(j, ex, k_slot)
                tp_high(i)

            for half in range(2):
                for c in range(NC):
                    act_e.wait_ge(xt_done, half * NC + c + 1)
                    nc.scalar.activation(xT_hi[:, c, half * HALF:(half + 1) * HALF], xbank[half][c], ACT.Copy).then_inc(xt_hi_done, 1)
            for half in range(2):
                rope_high(K_hi[:, 0, half * HALF:(half + 1) * HALF])
            for half in range(2):
                rope_high(Q_hi[:, 0, half * HALF:(half + 1) * HALF])
            n.add("unit", 6)
            exponent(0, 0)
            for i in range(3):
                step(0, i, extras(0, i, first=True), 0)
            with act_e.Fori(0, GROUPS - 1) as g:
                n.enter(g)
                k_slot = act_e.snap((g + 1) % 2)
                for j, i in loop_steps():
                    step(j, i, extras(j, i), k_slot)
            n.leave(GROUPS - 1)
            for j, i in last_steps():
                step(j, i, extras(j, i, last=True), 0, more=(j, i) != (REP - 1, NT - 1))
            for j, i in tail_steps():
                extra_high(j, tail_extras(i), 0)

            def norms():
                act_e.wait_ge(eps_done, 2)
                act_e.wait_ge(var_done, NT)
                nc.scalar.activation(spread[:], mean_var[:, :, 1], ACT.Sqrt, bias=eps_ln[:]).then_inc(std_done, 1)
                for t in range(NT):
                    act_e.wait_ge(ln_done, t + 1)
                    if t >= 2:
                        act_e.wait_ge(sq_done, t - 1)
                    nc.scalar.activation(V_stage[:, t % 2 * HID:(t % 2 + 1) * HID], y[:, t, :], ACT.Square,
                                         accum_out=sum_sq[:, t:t + 1]).then_inc(sq_done, 1)
                act_e.wait_ge(sq_done, NT)
                nc.scalar.activation(spread[:], sum_sq[:], ACT.Sqrt, bias=eps_rms[:], scale=1.0 / HID).then_inc(std_done, 1)
                for half in range(2):
                    for c in range(NC):
                        act_e.wait_ge(xt_done, 2 * NC + half * NC + c + 1)
                        nc.scalar.activation(xT_hi[:, c, half * HALF:(half + 1) * HALF], xbank[half][c], ACT.Copy,
                                             scale=ln_w_sb[:, c:c + 1]).then_inc(xt_hi_done, 1)

            tp_base = HEADS * 12

            def weight_high(dst, v, parity):
                act_e.wait_ge(tp_done, v + 1)
                nc.scalar.activation(dst, TP[:, parity].rearrange("p (a b) -> p a b", b=P), ACT.Copy).then_inc(tp_hi_done, 1)

            def gate_up_high(v0):
                for k, (w, i2) in enumerate(((gT, 0), (gT, 1), (uT, 0), (uT, 1))):
                    weight_high(w[0][:, :, i2 * P:(i2 + 1) * P], v0 + k, k % 2)

            def down_high(v0):
                for i2 in range(2):
                    weight_high(dT[0][:, i2].rearrange("p (a b) -> p a b", b=P), v0 + i2, i2 % 2)

            def activations(p):
                for u in range(4):
                    i2, half = divmod(u, 2)
                    act_e.wait_ge(gu_done, p * 4 + (u + 1))
                    nc.scalar.activation(rope_c[:, u % 2], S[:, u % 2, 0:HALF], ACT.Silu).then_inc(silu_done, 1)
                    act_e.wait_ge(prod_done, p * 4 + (u + 1))
                    nc.scalar.activation(act[0][:, i2, half * HALF:(half + 1) * HALF], rope_s[:, u % 2], ACT.Copy).then_inc(act_hi_done, 1)

            gate_up_high(tp_base)
            norms()
            with act_e.Fori(0, PAIRS - 1) as p:
                activations(p)
                gate_up_high(p * 6 + (tp_base + 4))
                down_high(p * 6 + (tp_base + 8))
            activations(PAIRS - 1)
            down_high(tp_base + (PAIRS - 1) * 6 + 4)

            act_e.wait_ge(var_done, 2 * NT)
            nc.scalar.activation(spread[:], mean_var[:, :, 1], ACT.Sqrt, bias=eps_ln[:]).then_inc(std_done, 1)

        @block.vector
        def _(dve):
            n = Tally()

            def maximum(i):
                slot, at = n.n["tile"] % 2, n.n["tile"] % 4
                dve.wait_ge(score_done, n["tile"] + 1)
                width = P * (i + 1)
                src = S[:, slot, 0:width]
                if width > 512:
                    src = S[:, slot].rearrange("p (a b) -> p a b", a=2)[:, :, 0:width // 2]
                if n.n["tile"] >= 4:
                    dve.wait_ge(exp_done, n["tile"] - 3)
                nc.vector.tensor_reduce(neg_max[:, at:at + 1], src, AX.XY if width > 512 else AX.X, ALU.max,
                                        negate=True).then_inc(max_done, 1)
                n.add("tile")

            def tp_low(i):
                for u in range(tp_banks(i)):
                    dve.wait_ge(tp_hi_done, n["pt"] + 1)
                    hi, src = pt_views(PT_hi, i, u, n.n["pt"] % 2)
                    lo, _ = pt_views(PT_lo, i, u, n.n["pt"] % 2)
                    nc.vector.tensor_tensor(lo, src, hi.bitcast(F32), ALU.subtract).then_inc(tp_lo_done, 1)
                    n.add("pt")

            def rope(half):
                bank, r = n.n["unit"] % 2, n.n["rope"] % 2
                cols = slice(half * HALF, (half + 1) * HALF)
                dve.wait_ge(unit_done, n["unit"] + 1)
                if n.n["rope"] >= 2:
                    dve.wait_ge(rope_sum_done, n["rope"] - 1)
                nc.vector.tensor_tensor(rope_c[:, r], ACC[:, bank], cos_sb[:, cols], ALU.mult)
                h = HD // 2
                nc.vector.tensor_tensor(rope_s[0:h, r], ACC[h:P, bank], sin_sb[h:P, cols], ALU.mult)
                nc.vector.tensor_tensor(rope_s[h:P, r], ACC[0:h, bank], sin_sb[0:h, cols], ALU.mult).then_inc(unit_free, 1)
                n.add("rope")
                n.add("unit")

            def unit_low(hi, lo):
                dve.wait_ge(unit_hi_done, n["ohi"] + 1)
                nc.vector.tensor_tensor(lo, ACC[:, n.n["unit"] % 2], hi.bitcast(F32), ALU.subtract).then_inc(unit_free, 1)
                n.add("ohi")
                n.add("unit")

            def reciprocals(head, half):
                rows = slice(half * HT, (half + 1) * HT)
                nc.vector.reciprocal(row_rcp[:, head % 2, rows], row_sum[:, head % 2, rows]).then_inc(rcp_done, 1)
                n.add("recip")

            def extra(j, i, ex):
                head = j if i >= 3 else j - 1
                for kind, a in ex:
                    if kind in "qk":
                        rope(a)
                    if kind == "v":
                        dve.wait_ge(unit_done, n["unit"] + 1)
                        nc.vector.tensor_copy(V_stage[:, a * HALF:(a + 1) * HALF], ACC[:, n.n["unit"] % 2]).then_inc(unit_free, 1)
                        n.add("unit")
                    if kind == "vt":
                        tiles = slice(a * HT, (a + 1) * HT)
                        unit_low(V_hi[:, tiles, :].rearrange("p a b -> p (a b)"), V_lo[:, tiles, :].rearrange("p a b -> p (a b)"))
                    if kind == "pv":
                        unit_low(O_hi[:, a * HALF:(a + 1) * HALF], O_lo[:, a * HALF:(a + 1) * HALF])
                        reciprocals(head, a)
                    if kind == "y":
                        dve.wait_ge(unit_done, n["unit"] + 1)
                        dve.wait_ge(rcp_done, n["recip"])
                        nc.vector.scalar_tensor_tensor(out=y[:, a, :], in0=ACC[:, n.n["unit"] % 2],
                                                       scalar=row_rcp[:, head % 2, a:a + 1], in1=y[:, a, :],
                                                       op0=ALU.mult, op1=ALU.add).then_inc(unit_free, 1)
                        n.add("unit")

            def step(j, i, ex, more=True):
                if more:
                    maximum((i + 1) % NT)
                extra(j, i, ex)
                tp_low(i)

            nc.vector.memset(eps_ln[:], LN_EPS).then_inc(eps_done, 1)
            nc.vector.memset(eps_rms[:], RMS_EPS).then_inc(eps_done, 1)
            for half in range(2):
                for c in range(NC):
                    dve.wait_ge(xt_hi_done, half * NC + c + 1)
                    cols = slice(half * HALF, (half + 1) * HALF)
                    nc.vector.tensor_tensor(xT_lo[:, c, cols], xbank[half][c], xT_hi[:, c, cols].bitcast(F32), ALU.subtract).then_inc(xt_lo_done, 1)
            dve.wait_ge(table_in, 48)
            rope(0)
            rope(1)
            extra(0, 6, [("v", 0), ("v", 1)])
            rope(0)
            rope(1)
            maximum(0)
            for i in range(3):
                step(0, i, extras(0, i, first=True))
            with dve.Fori(0, GROUPS - 1) as g:
                n.enter(g)
                for j, i in loop_steps():
                    step(j, i, extras(j, i))
            n.leave(GROUPS - 1)
            for j, i in last_steps():
                step(j, i, extras(j, i, last=True), more=(j, i) != (REP - 1, NT - 1))
            for j, i in tail_steps():
                extra(j, i, tail_extras(i))

            tp_base, unit_base = HEADS * 12, n.n["unit"]

            def weight_low(w, v, parity):
                hi, lo = w
                dve.wait_ge(tp_hi_done, v + 1)
                nc.vector.tensor_tensor(lo, TP[:, parity].rearrange("p (a b) -> p a b", b=P), hi.bitcast(F32),
                                        ALU.subtract).then_inc(tp_lo_done, 1)

            def gate_up_low(v0):
                for k, (w, i2) in enumerate(((gT, 0), (gT, 1), (uT, 0), (uT, 1))):
                    weight_low([a[:, :, i2 * P:(i2 + 1) * P] for a in w], v0 + k, k % 2)

            def down_low(v0):
                for i2 in range(2):
                    weight_low([a[:, i2].rearrange("p (a b) -> p a b", b=P) for a in dT], v0 + i2, i2 % 2)

            def products(p, first=False):
                for u in range(4):
                    dve.wait_ge(silu_done, p * 4 + (u + 1))
                    if u >= 2 or not first:
                        dve.wait_ge(act_lo_done, p * 4 + (u - 1))
                    nc.vector.tensor_tensor(rope_s[:, u % 2], S[:, u % 2, HALF:2 * HALF], rope_c[:, u % 2],
                                            ALU.mult).then_inc(prod_done, 1)

            def down_add(p):
                for t in range(NT):
                    dve.wait_ge(unit_done, p * NT + (unit_base + t + 1))
                    nc.vector.tensor_tensor(y[:, t, :], ACC[:, t % 2], y[:, t, :], ALU.add).then_inc(unit_free, 1)

            def variances(t, rows_done):
                dve.wait_ge(unit_free, rows_done)
                nc.vector.bn_stats(stats[:, t, :], y[:, t, :]).then_inc(stats_done, 1)
                n.add("stats")
                dve.wait_ge(stats_done, n["stats"])
                nc.vector.bn_aggr(mean_var[:, t, :], stats[:, t, :]).then_inc(var_done, 1)

            def inverses(turn):
                dve.wait_ge(std_done, turn)
                nc.vector.reciprocal(inv_spread[:], spread[:]).then_inc(inv_done, 1)
                dve.wait_ge(inv_done, turn)

            def layer_norm(t):
                return nc.vector.tensor_scalar(y[:, t, :], y[:, t, :], mean_var[:, t, 0:1], inv_spread[:, t:t + 1],
                                               ALU.subtract, ALU.mult)

            gate_up_low(tp_base)
            for t in range(NT):
                variances(t, unit_base)
            inverses(1)
            for t in range(NT):
                layer_norm(t).then_inc(ln_done, 1)
            inverses(2)
            for t in range(NT):
                nc.vector.tensor_scalar(nx[t], y[:, t, :], inv_spread[:, t:t + 1], None, ALU.mult).then_inc(nx_done, 1)
            for half in range(2):
                for c in range(NC):
                    dve.wait_ge(xt_hi_done, 2 * NC + half * NC + c + 1)
                    cols = slice(half * HALF, (half + 1) * HALF)
                    nc.vector.scalar_tensor_tensor(out=xT_lo[:, c, cols], in0=xbank[half][c], scalar=ln_w_sb[:, c:c + 1],
                                                   in1=xT_hi[:, c, cols].bitcast(F32), op0=ALU.mult,
                                                   op1=ALU.subtract).then_inc(xt_lo_done, 1)

            products(0, first=True)
            gate_up_low(tp_base + 4)
            down_low(tp_base + 8)
            down_add(0)
            with dve.Fori(1, PAIRS - 1) as p:
                products(p)
                gate_up_low(p * 6 + (tp_base + 4))
                down_low(p * 6 + (tp_base + 8))
                down_add(p)
            products(PAIRS - 1)
            down_low(tp_base + (PAIRS - 1) * 6 + 4)
            down_add(PAIRS - 1)

            for t in range(NT):
                variances(t, unit_base + (PAIRS - 1) * NT + t + 1)
            inverses(3)
            for t in range(NT):
                layer_norm(t).then_inc(out_ready, 1)

        @block.tensor
        def _(pe):
            n = Tally()
            at = {}

            def product(dst, a, b, start, stop):
                nc.tensor.matmul(dst, a[0], b[0], start=start, stop=False)
                nc.tensor.matmul(dst, a[0], b[1], start=False, stop=False)
                return nc.tensor.matmul(dst, a[1], b[0], start=False, stop=stop)

            def scores(j, i, k_slot):
                slot = n.n["tile"] % 2
                if i % HT == 0:
                    pe.wait_ge(rope_lo_done, n.at("rope", at["q", i // HT]) if i == 0 else n["rope"])
                if n.n["tile"] >= 2:
                    pe.wait_ge(exp_done, n["tile"] - 1)
                q = [a[:, j % 2, i * P:(i + 1) * P] for a in (Q_hi, Q_lo)]
                for col, key, width in score_chunks(i):
                    dst = S[:, slot, col:col + width]
                    k = [a[:, bass.ds(k_slot, 1), key:key + width].rearrange("p a b -> p (a b)") for a in (K_hi, K_lo)]
                    nc.tensor.matmul(dst, q[0], k[0], start=True, stop=False)
                    if key + width == P * (i + 1):
                        nc.tensor.matmul(S[:, slot, col + width - P:col + width], ident_bf[:], mask_bf[:],
                                         start=False, stop=False)
                    nc.tensor.matmul(dst, q[0], k[1], start=False, stop=False)
                    last = nc.tensor.matmul(dst, q[1], k[0], start=False, stop=True)
                last.then_inc(score_done, 1)
                n.add("tile")

            def transposes(i, tile):
                pe.wait_ge(exp_done, n.at("tile", tile + 1))
                for u in range(tp_banks(i)):
                    bank = n.n["pt"] % 2
                    if n.n["pt"] >= 2:
                        pe.wait_ge(tp_lo_done, n["pt"] - 1)
                    for b in range(4 * u, min(4 * u + 4, i + 1)):
                        last = nc.tensor.transpose(TP[:, bank, (b % 4) * P:(b % 4 + 1) * P],
                                                   probs[:, tile % 2, b * P:(b + 1) * P], ident[:])
                    last.then_inc(tp_done, 1)
                    n.add("pt")
                at["pt", i] = n.n["pt"]

            def unit():
                if n.n["unit"] >= 2:
                    pe.wait_ge(unit_free, n["unit"] - 1)
                bank = ACC[:, n.n["unit"] % 2]
                n.add("unit")
                return bank

            def project(w, half):
                acc = unit()
                cols = slice(half * HALF, (half + 1) * HALF)
                for c in range(NC):
                    last = product(acc, [a[:, c, :] for a in w], [a[:, c, cols] for a in (xT_hi, xT_lo)],
                                   c == 0, c == NC - 1)
                last.then_inc(unit_done, 1)

            def extra(ex):
                for kind, a in ex:
                    if kind == "q":
                        pe.wait_ge(wq_done, n["wq"] + 1)
                        project((wq_hi, wq_lo), a)
                        n.add("rope")
                        at["q", a] = n.n["rope"]
                        n.add("wq", a)
                    if kind in "kv":
                        pe.wait_ge(wkv_done, n["wkv"] + 1)
                        project((wkv_hi, wkv_lo), a)
                        n.add("rope", kind == "k")
                        n.add("wkv", a)
                    if kind == "vt":
                        acc = unit()
                        for b in range(HT):
                            key = (a * HT + b) * P
                            last = nc.tensor.transpose(acc[:, b * P:(b + 1) * P], V_stage[:, key:key + P], ident[:])
                        last.then_inc(unit_done, 1)
                    if kind == "pv":
                        pe.wait_ge(tp_lo_done, n.at("pt", at["pt", HT * (a + 1) - 1]))
                        acc = unit()
                        keys = HT * (a + 1)
                        for k in range(keys):
                            skip = max(0, k - HT * a) * P
                            row = HT * a + k
                            last = product(acc[:, skip:HALF], [v[:, k, :] for v in (V_hi, V_lo)],
                                           [p[:, row, skip:HALF] for p in (PT_hi, PT_lo)], k == 0, k == keys - 1)
                        last.then_inc(unit_done, 1)
                        at["pv"] = n.n["unit"]
                    if kind == "y":
                        if a % HT == 0:
                            pe.wait_ge(unit_free, n.at("unit", at["pv"]))
                        pe.wait_ge(wo_done, n["wo"] + 1)
                        acc = unit()
                        cols = slice(a * P, (a + 1) * P)
                        product(acc, (O_hi[:, cols], O_lo[:, cols]), (wo_hi[:], wo_lo[:]), True, True).then_inc(unit_done, 1)
                        n.add("wo", a == NT - 1)

            def step(j, i, ex, slots, more=True):
                tile = n.n["tile"] - 1
                if more:
                    following = j + (i + 1) // NT
                    scores(following, (i + 1) % NT, slots[following // REP])
                extra(ex)
                transposes(i, tile)

            def transpose_rows(src):
                for half in range(2):
                    for c in range(NC):
                        for t in range(HT):
                            last = nc.tensor.transpose(xbank[half][c][:, t * P:(t + 1) * P],
                                                       src(half * HT + t)[:, c * P:(c + 1) * P], ident[:])
                        last.then_inc(xt_done, 1)

            pe.wait_ge(const_done, 7)
            pe.wait_ge(x_in, 16)
            transpose_rows(lambda t: y[:, t, :])
            pe.wait_ge(xt_lo_done, 2 * NC)
            extra([("k", 0), ("k", 1), ("v", 0), ("v", 1), ("q", 0), ("q", 1)])
            scores(0, 0, 0)
            for i in range(3):
                step(0, i, extras(0, i, first=True), (0, 0))
            with pe.Fori(0, GROUPS - 1) as g:
                n.enter(g)
                slots = (pe.snap(g % 2), pe.snap((g + 1) % 2))
                for j, i in loop_steps():
                    step(j, i, extras(j, i), slots)
            n.leave(GROUPS - 1)
            for j, i in last_steps():
                step(j, i, extras(j, i, last=True), ((GROUPS - 1) % 2, 0), more=(j, i) != (REP - 1, NT - 1))
            for j, i in tail_steps():
                extra(tail_extras(i))

            tp_base, unit_base = HEADS * 12, n.n["unit"]

            def weight_transposes(raw, blocks, v):
                pe.wait_ge(tp_lo_done, v - 1)
                for b, block in enumerate(blocks):
                    last = nc.tensor.transpose(TP[:, raw % 2, b * P:(b + 1) * P], block, ident[:])
                last.then_inc(tp_done, 1)

            def gate_up_transposes(p, v0):
                pe.wait_ge(gate_in, p * 16 + 16)
                pe.wait_ge(up_in, p * 16 + 16)
                for k in range(4):
                    raw = (gate_raw, up_raw)[k // 2]
                    weight_transposes(k, [raw[:, k % 2, c * P:(c + 1) * P] for c in range(NC)], v0 + k)

            def down_transposes(p, v0):
                pe.wait_ge(down_in, p * 16 + 16)
                for i2 in range(2):
                    weight_transposes(i2, [down_raw[:, c, i2 * P:(i2 + 1) * P] for c in range(NC)], v0 + i2)

            def gate_up(p, first=False):
                pe.wait_ge(tp_lo_done, p * 6 + (tp_base + 4))
                for u in range(4):
                    i2, half = divmod(u, 2)
                    if u >= 2 or not first:
                        pe.wait_ge(prod_done, p * 4 + (u - 1))
                    cols, rows = slice(half * HALF, (half + 1) * HALF), slice(i2 * P, (i2 + 1) * P)
                    for bank, w in enumerate((gT, uT)):
                        for c in range(NC):
                            last = product(S[:, u % 2, bank * HALF:(bank + 1) * HALF], [a[:, c, rows] for a in w],
                                           [a[:, c, cols] for a in (xT_hi, xT_lo)], c == 0, c == NC - 1)
                    last.then_inc(gu_done, 1)

            def down(p, split):
                pe.wait_ge(tp_lo_done, split)
                pe.wait_ge(act_lo_done, p * 4 + 4)
                for t in range(NT):
                    pe.wait_ge(unit_free, p * NT + (unit_base + t - 1))
                    cols = slice(t * P, (t + 1) * P)
                    for i2 in range(2):
                        last = product(ACC[:, t % 2], [a[:, i2, cols] for a in act], [a[:, i2, :] for a in dT], i2 == 0, i2 == 1)
                    last.then_inc(unit_done, 1)

            gate_up_transposes(0, tp_base)
            pe.wait_ge(nx_done, NT)
            pe.wait_ge(tp_lo_done, tp_base + 4)
            transpose_rows(lambda t: nx[t])
            pe.wait_ge(xt_lo_done, 4 * NC)
            gate_up(0, first=True)
            gate_up_transposes(1, tp_base + 4)
            down_transposes(0, tp_base + 8)
            down(0, tp_base + 10)
            with pe.Fori(1, PAIRS - 1) as p:
                gate_up(p)
                gate_up_transposes(p + 1, p * 6 + (tp_base + 4))
                down_transposes(p, p * 6 + (tp_base + 8))
                down(p, p * 6 + (tp_base + 10))
            gate_up(PAIRS - 1)
            down_transposes(PAIRS - 1, tp_base + (PAIRS - 1) * 6 + 4)
            down(PAIRS - 1, tp_base + (PAIRS - 1) * 6 + 6)


def rope_tables():
    import numpy as np
    theta, factor, hi_ff, lo_ff, orig_max = 500000.0, 8.0, 4.0, 1.0, 1024
    inv = 1.0 / theta ** (np.arange(0, HD, 2, dtype=np.float64) / HD)
    wavelen = 2.0 * np.pi / inv
    low_wl, high_wl = orig_max / lo_ff, orig_max / hi_ff
    smooth = (orig_max / wavelen - lo_ff) / (hi_ff - lo_ff)
    scaled = np.where(wavelen > low_wl, inv / factor, inv)
    mid = (wavelen <= low_wl) & (wavelen >= high_wl)
    scaled = np.where(mid, (1 - smooth) * inv / factor + smooth * inv, scaled).astype(np.float32)
    freqs = np.arange(T, dtype=np.float32)[None, :] * scaled[:, None]
    scale = float(HD) ** -0.25
    cos = np.cos(freqs).astype(np.float64) * scale
    sin = np.sin(freqs).astype(np.float64) * scale
    return (np.concatenate([cos, cos]).astype(np.float32), np.concatenate([sin, -sin]).astype(np.float32))


_INS = ['L0_attn_x', 'L0_attn_wq', 'L0_attn_wk', 'L0_attn_wv', 'L0_attn_wo',
        'L0_ffn_ln_w', 'L0_ffn_gate_w', 'L0_ffn_up_w', 'L0_ffn_down_w']


def kernel(**inputs):
    import numpy as np
    import concourse.bacc as bacc
    from concourse.bass_utils import run_bass_kernel_spmd

    nc = bacc.Bacc("TRN2", target_bir_lowering=False, num_devices=1)
    arrays, args = {}, []
    for name in _INS:
        arrays[f"in_{name}_dram"] = np.ascontiguousarray(inputs[name])
    for name, table in zip(("cos", "sin"), rope_tables()):
        arrays[f"in_{name}_dram"] = table
    for name, a in arrays.items():
        args.append(nc.dram_tensor(name, a.shape, mybir.dt.from_np(a.dtype), kind="ExternalInput").ap())
    args.append(nc.dram_tensor("out_0_dram", (1, T, HID), F32, kind="ExternalOutput").ap())
    layer_kernel(nc, *args)
    r = run_bass_kernel_spmd(nc, [arrays], core_ids=[0])
    return r.results[0]["out_0_dram"]
```

```python
from contextlib import ExitStack

import concourse.bass as bass
from concourse import mybir

F32 = mybir.dt.float32
F32R = mybir.dt.float32r
BF16 = mybir.dt.bfloat16
ALU = mybir.AluOpType
ACT = mybir.ActivationFunctionType
AX = mybir.AxisListType

P = 128
HEADS, KV_HEADS, HD = 32, 8, 128
T, HID, INTER = 1024, 512, 1792
REP = HEADS // KV_HEADS
NT = T // P
NC = HID // P
HALF = T // 2
HT = NT // 2
GROUPS = KV_HEADS
PAIRS = INTER // (2 * P)
LN_EPS = 1e-5
RMS_EPS = 1e-5
MASKED = -3.0e38


class Tally:

    PER = {
        "tile": REP * NT,
        "pt": REP * 12,
        "x": REP * 4 + 6,
        "copy": REP * 2 + 4,
        "split": REP * 2 + 2,
        "y": REP * NT,
        "rope": REP * 2 + 2,
        "recip": REP * 2,
        "wq": REP, "wo": REP, "wkv": 2,
        "stats": 0,
    }

    def __init__(self):
        self.n = dict.fromkeys(self.PER, 0)
        self.marks = {}
        self.group = 0

    def __getitem__(self, kind):
        return self.n[kind] + self.PER[kind] * self.group

    def at(self, kind, local):
        return local + self.PER[kind] * self.group

    def mark(self, name, kind):
        self.marks[name] = (kind, self.n[kind])

    def marked(self, name):
        return self.at(*self.marks[name])

    def add(self, kind, count=1):
        self.n[kind] += count

    def enter(self, group):
        self.group = group

    def leave(self, iterations):
        self.group = 0
        for kind, per in self.PER.items():
            self.n[kind] += per * (iterations - 1)
        for name, (kind, local) in self.marks.items():
            self.marks[name] = (kind, local + self.PER[kind] * (iterations - 1))


def products(kind, half):
    return {"pv": HT * (half + 1), "vt": HT}.get(kind, NC)


def extras(j, i, last=False):
    heads = REP if last else 2 * REP
    if j == 0 and i in (0, 1):
        return [("q", i, 1, 0, NC)]
    if i == 0 and j + 1 < heads:
        return [("q", 1, j + 1, 0, NC)]
    if i == 7 and j + 2 < heads:
        return [("q", 0, j + 2, 0, NC)]
    if i in (1, 2) and j > 0:
        return [("pv", 1, j - 1, (i - 1) * HT, i * HT)]
    if i in (3, 4) and j % REP == 0:
        return [("vt", i - 3, j, 0, HT)]
    if i in (3, 4) and j < REP - 1 and not last:
        return [("k", j - 1, REP, (i - 3) * NC // 2, (i - 2) * NC // 2)]
    if i in (3, 4) and not last:
        return [("v", i - 3, REP, 0, NC)]
    if i == 5:
        return [("pv", 0, j, 0, 1)]
    if i == 6:
        return [("pv", 0, j, 1, HT)]
    return []


def finished(j, i, last=False):
    return [(kind, half, head) for kind, half, head, _, end in extras(j, i, last) if end == products(kind, half)]


ROPE_STEPS = {"q": {"sin0": 0, "sin1": 0, "add": 1, "high": 1, "low": 2},
              "k": {"sin0": 0, "sin1": 1, "add": 2, "high": 2, "low": 3}}


def ropes_due(stage, j, i, last=False):
    def projected(ago):
        jj, ii = divmod(j * NT + i - ago, NT)
        return [unit for unit in (finished(jj, ii, last) if jj >= 0 else []) if unit[0] in "qk"]

    due = []
    for ago in range(max(steps[stage] for steps in ROPE_STEPS.values()), -1, -1):
        for kind, half, head in projected(ago):
            if ROPE_STEPS[kind][stage] == ago:
                before = sum(len(projected(a)) for a in range(1, ago))
                due.append((kind, half, head, before, before + (len(projected(0)) if ago else 0)))
    return due


FIRST_HEAD = [(0, i) for i in range(NT)]
LOOP_STEPS = [(j, i) for j in range(1, REP + 1) for i in range(NT)]
LAST_STEPS = [(j, i) for j in range(1, REP) for i in range(NT)]
START = [("q", 0), ("k", 0), ("k", 1), ("v", 0), ("v", 1), ("q", 1)]


def y_bank(t, tail=False):
    return t % 2 if tail and t >= 2 else 1


def tp_banks(i):
    return i // 4 + 1


def score_chunks(i):
    width = P * (i + 1)
    if width <= 512:
        return [(0, 0, width)]
    return [(0, 0, width // 2), (512, width // 2, width // 2)]


def layer_kernel(nc, x, wq, wk, wv, wo, ln_w, gate_w, up_w, down_w, cos_t, sin_t, out):
    x_v = x.rearrange("b (i p) d -> p (b i) d", p=P)
    out_v = out.rearrange("b (i p) d -> p (b i) d", p=P)
    wq_v = wq.rearrange("(c p) n -> p c n", p=P)
    wk_v = wk.rearrange("(c p) n -> p c n", p=P)
    wv_v = wv.rearrange("(c p) n -> p c n", p=P)
    ln_w_v = ln_w.rearrange("(c p) -> p c", p=P)
    down_v = down_w.rearrange("(n p) i -> p n i", p=P)

    with ExitStack() as ctx:
        def sb(name, shape, dt=F32):
            return ctx.enter_context(nc.sbuf_tensor(name, [P] + shape, dt))

        def sem(name):
            return ctx.enter_context(nc.semaphore(name))

        y = sb("y", [NT, HID])
        xT_hi, xT_lo = sb("xT_hi", [NC, T], F32R), sb("xT_lo", [NC, T], F32R)
        PT_hi, PT_lo = sb("PT_hi", [12, HALF], F32R), sb("PT_lo", [12, HALF], F32R)
        Q_hi, Q_lo = sb("Q_hi", [2, T], F32R), sb("Q_lo", [2, T], F32R)
        K_hi, K_lo = sb("K_hi", [2, T], F32R), sb("K_lo", [2, T], F32R)
        V_hi, V_lo = sb("V_hi", [NT, HD], F32R), sb("V_lo", [NT, HD], F32R)
        O_hi, O_lo = sb("O_hi", [T], F32R), sb("O_lo", [T], F32R)
        V_stage = sb("V_stage", [T])
        cos_sb, sin_sb = sb("cos_sb", [T]), sb("sin_sb", [T])
        wq_raw, wq_hi, wq_lo = sb("wq_raw", [NC, HD]), sb("wq_hi", [NC, HD], F32R), sb("wq_lo", [NC, HD], F32R)
        wkv_raw, wkv_hi, wkv_lo = sb("wkv_raw", [NC, HD]), sb("wkv_hi", [NC, HD], F32R), sb("wkv_lo", [NC, HD], F32R)
        wo_raw, wo_hi, wo_lo = sb("wo_raw", [HID]), sb("wo_hi", [2, HID], F32R), sb("wo_lo", [2, HID], F32R)
        probs = sb("probs", [2, T])
        qk_raw, rope_c, rope_s = sb("qk_raw", [2, HALF]), sb("rope_c", [2, HALF]), sb("rope_s", [2, HALF])
        gate_raw, up_raw = sb("gate_raw", [2, HID]), sb("up_raw", [2, HID])
        ident = sb("ident", [P])
        ident_bf, mask_bf = sb("ident_bf", [P], BF16), sb("mask_bf", [P], BF16)
        neg_max = sb("neg_max", [4])
        row_sum, row_rcp = sb("row_sum", [2, NT]), sb("row_rcp", [2, NT])
        ln_w_sb = sb("ln_w_sb", [NC])
        stats, mean_var, sum_sq = sb("stats", [NT, 6]), sb("mean_var", [NT, 2]), sb("sum_sq", [NT])
        spread, inv_spread = sb("spread", [NT]), sb("inv_spread", [NT])
        zero = sb("zero", [1])
        eps_ln, eps_rms = sb("eps_ln", [1]), sb("eps_rms", [1])

        def part(tensor, at, shape):
            size = shape[0] * shape[1]
            flat = tensor[:].rearrange("p a b -> p (a b)")[:, at:at + size]
            return flat.rearrange("p (a b) -> p a b", b=shape[1])

        gT = [part(t, 0, (NC, 2 * P)) for t in (PT_hi, PT_lo)]
        uT = [part(t, NC * 2 * P, (NC, 2 * P)) for t in (PT_hi, PT_lo)]
        dT = [part(t, NC * 4 * P, (2, HID)) for t in (PT_hi, PT_lo)]
        act = [part(t, NC * 4 * P + 2 * HID, (2, T)) for t in (PT_hi, PT_lo)]
        nx = [b[:, k * HID:(k + 1) * HID] for b in (cos_sb, sin_sb) for k in range(2)]
        nx += [qk_raw[:, 0], qk_raw[:, 1]] + [w[:].rearrange("p a b -> p (a b)") for w in (wq_raw, wkv_raw)]
        down_raw = part(probs, 0, (NC, 2 * P))

        S = ctx.enter_context(nc.psum_tensor("S", [P, 2, T], F32))
        TP = ctx.enter_context(nc.psum_tensor("TP", [P, 2, HALF], F32))
        ACC = ctx.enter_context(nc.psum_tensor("ACC", [P, 2, HALF], F32))
        xbank = [[S[:, c // 2, (c % 2) * HALF:(c % 2 + 1) * HALF] for c in range(NC)],
                 [TP[:, 0], TP[:, 1], ACC[:, 0], ACC[:, 1]]]

        def pt_views(dst, i, u, bank):
            blocks = min(4, i + 1 - 4 * u)
            row = (0 if i < HT else HT) + 4 * u
            col = (i % HT) * P
            return dst[:, row:row + blocks, col:col + P], TP[:, bank, 0:blocks * P].rearrange("p (a b) -> p a b", b=P)

        x_in = [sem("x_in0"), sem("x_in1")]
        cos_in, sin_in, ln_w_in = sem("cos_in"), sem("sin_in"), sem("ln_w_in")
        wq_in, wkv_in, wo_in = sem("wq_in"), sem("wkv_in"), sem("wo_in")
        gate_in, up_in, down_in = sem("gate_in"), sem("up_in"), sem("down_in")
        const_done = sem("const_done")
        w_hi_done = sem("w_hi_done")
        wq_done, wkv_done, wo_done = sem("wq_done"), sem("wkv_done"), sem("wo_done")
        xt_done, xt_hi_done, xt_lo_done = sem("xt_done"), sem("xt_hi_done"), sem("xt_lo_done")
        score_done = sem("score_done")
        max_done = sem("max_done")
        exp_done = sem("exp_done")
        tp_done = sem("tp_done")
        tp_hi_done = sem("tp_hi_done")
        tp_lo_done = sem("tp_lo_done")
        x_done = sem("x_done")
        copy_done = sem("copy_done")
        split_hi_done = sem("split_hi_done")
        split_done = sem("split_done")
        y_done = sem("y_done")
        y_free = sem("y_free")
        rope_c_done = sem("rope_c_done")
        rope_s_done = sem("rope_s_done")
        rope_sum_done = sem("rope_sum_done")
        rope_hi_done = sem("rope_hi_done")
        rope_lo_done = sem("rope_lo_done")
        rcp_done = sem("rcp_done")
        stats_done = sem("stats_done")
        var_done = sem("var_done")
        std_done = sem("std_done")
        inv_done = sem("inv_done")
        ln_done = sem("ln_done")
        sq_done = sem("sq_done")
        nx_done = sem("nx_done")
        gu_done = sem("gu_done")
        silu_done = sem("silu_done")
        prod_done = sem("prod_done")
        act_hi_done = sem("act_hi_done")
        act_lo_done = sem("act_lo_done")
        out_ready, out_done = sem("out_ready"), sem("out_done")
        eps_done = sem("eps_done")

        block = ctx.enter_context(nc.Block())

        @block.sync
        def _(sp):
            for half in range(2):
                rows = slice(half * HT, (half + 1) * HT)
                sp.dma_start(y[:, rows, :], x_v[:, rows, :]).then_inc(x_in[half], 16)
                if half == 0:
                    sp.dma_start(wq_raw[:], wq_v[:, :, 0:HD]).then_inc(wq_in, 16)
                    sp.dma_start(wkv_raw[:], wk_v[:, :, 0:HD]).then_inc(wkv_in, 16)
            sp.dma_start(cos_sb[:], cos_t).then_inc(cos_in, 16)
            sp.dma_start(sin_sb[:], sin_t).then_inc(sin_in, 16)
            sp.wait_ge(wkv_done, 1)
            sp.dma_start(wkv_raw[:], wv_v[:, :, 0:HD]).then_inc(wkv_in, 16)
            with nc.allow_non_contiguous_dma(reason="512 words, once"):
                sp.dma_start(ln_w_sb[:], ln_w_v).then_inc(ln_w_in, 16)
            sp.dma_start(wo_raw[:], wo[0:HD, :]).then_inc(wo_in, 16)
            sp.dma_start(gate_raw[:], gate_w[0:2 * P, :].rearrange("(a p) k -> p a k", p=P)).then_inc(gate_in, 16)
            sp.dma_start(up_raw[:], up_w[0:2 * P, :].rearrange("(a p) k -> p a k", p=P)).then_inc(up_in, 16)

            def load_wq(h):
                sp.wait_ge(wq_done, h)
                sp.dma_start(wq_raw[:], wq_v[:, :, bass.ds(h * HD, HD)]).then_inc(wq_in, 16)

            def load_wo(h):
                sp.wait_ge(wo_done, h)
                sp.dma_start(wo_raw[:], wo[bass.ds(h * HD, HD), :]).then_inc(wo_in, 16)

            load_wq(1)
            load_wq(2)
            with sp.Fori(0, GROUPS - 1) as g:
                for j in range(1, REP + 1):
                    if j == 1:
                        sp.wait_ge(wkv_done, g * 2 + 2)
                        sp.dma_start(wkv_raw[:], wk_v[:, :, bass.ds(g * HD + HD, HD)]).then_inc(wkv_in, 16)
                    if j == 2:
                        sp.wait_ge(wkv_done, g * 2 + 3)
                        sp.dma_start(wkv_raw[:], wv_v[:, :, bass.ds(g * HD + HD, HD)]).then_inc(wkv_in, 16)
                    load_wo(g * REP + j)
                    load_wq(g * REP + (j + 2))
            for h in range((GROUPS - 1) * REP + 1, HEADS):
                load_wo(h)
                if h + 2 < HEADS:
                    load_wq(h + 2)

            tp_base = HEADS * 12

            def load_gate_up(p):
                sp.wait_ge(tp_done, p * 6 + (tp_base - 2))
                rows = bass.ds(p * 2 * P, 2 * P)
                sp.dma_start(gate_raw[:], gate_w[rows, :].rearrange("(a p) k -> p a k", p=P)).then_inc(gate_in, 16)
                sp.dma_start(up_raw[:], up_w[rows, :].rearrange("(a p) k -> p a k", p=P)).then_inc(up_in, 16)

            def load_down(p):
                sp.wait_ge(tp_done, p * 6 + tp_base)
                sp.dma_start(down_raw, down_v[:, :, bass.ds(p * 2 * P, 2 * P)]).then_inc(down_in, 16)

            load_down(0)
            load_gate_up(1)
            with sp.Fori(1, PAIRS - 1) as p:
                load_down(p)
                load_gate_up(p + 1)
            load_down(PAIRS - 1)

            for t in range(NT):
                sp.wait_ge(out_ready, t + 1)
                sp.dma_start(out_v[:, t, :], y[:, t, :]).then_inc(out_done, 16)
            sp.wait_ge(out_done, 16 * NT)

        @block.gpsimd
        def _(pool):
            n = Tally()

            nc.gpsimd.memset(ident[:], 0.0).then_inc(const_done, 1)
            nc.gpsimd.memset(ident_bf[:], 0.0).then_inc(const_done, 1)
            nc.gpsimd.memset(mask_bf[:], 0.0).then_inc(const_done, 1)
            nc.gpsimd.memset(zero[:], 0.0).then_inc(const_done, 1)
            pool.wait_ge(const_done, 4)
            for m in (ident, ident_bf):
                nc.gpsimd.affine_select(out=m[:], in_=m[:], compare_op=ALU.not_equal, fill=1.0, base=0,
                                        pattern=[[-1, P]], channel_multiplier=1).then_inc(const_done, 1)
            nc.gpsimd.affine_select(out=mask_bf[:], in_=mask_bf[:], compare_op=ALU.is_ge, fill=MASKED, base=0,
                                    pattern=[[-1, P]], channel_multiplier=1).then_inc(const_done, 1)
            def split(kind, raw, hi, lo, arrived, done):
                pool.wait_ge(arrived, n[kind] * 16 + 16)
                nc.gpsimd.tensor_tensor(hi, raw, zero[:, 0:1].to_broadcast([P, NC * HD]), ALU.add).then_inc(w_hi_done, 1)
                pool.wait_ge(w_hi_done, n["wq"] + n["wo"] + n["wkv"] + 1)
                nc.gpsimd.tensor_tensor(lo, raw, hi.bitcast(F32), ALU.subtract).then_inc(done, 1)
                n.add(kind)

            def flat(a):
                return a[:].rearrange("p a b -> p (a b)")

            def split_wq():
                split("wq", flat(wq_raw), flat(wq_hi), flat(wq_lo), wq_in, wq_done)

            def split_wkv():
                split("wkv", flat(wkv_raw), flat(wkv_hi), flat(wkv_lo), wkv_in, wkv_done)

            def split_wo():
                slot = n.n["wo"] % 2
                split("wo", wo_raw[:], wo_hi[:, slot], wo_lo[:, slot], wo_in, wo_done)

            def rope_cos(half):
                r, cols = n.n["rope"] % 2, slice(half * HALF, (half + 1) * HALF)
                pool.wait_ge(copy_done, n["copy"] + 1)
                if n.n["rope"] >= 2:
                    pool.wait_ge(rope_lo_done, n["rope"] - 1)
                nc.gpsimd.tensor_tensor(rope_c[:, r], qk_raw[:, r], cos_sb[:, cols], ALU.mult).then_inc(rope_c_done, 1)
                n.add("rope")

            def rope_add(ago=0):
                r = (n.n["rope"] - 1 - ago) % 2
                pool.wait_ge(rope_c_done, n["rope"] - ago)
                pool.wait_ge(rope_s_done, (n["rope"] - ago) * 2)
                nc.gpsimd.tensor_tensor(rope_c[:, r], rope_c[:, r], rope_s[:, r], ALU.add).then_inc(rope_sum_done, 1)

            def rope_low(hi, lo, ago=0):
                r = (n.n["rope"] - 1 - ago) % 2
                pool.wait_ge(rope_hi_done, n["rope"] - ago)
                nc.gpsimd.tensor_tensor(lo, rope_c[:, r], hi.bitcast(F32), ALU.subtract).then_inc(rope_lo_done, 1)

            def half_of(a, slot, half):
                return a[:, slot, half * HALF:(half + 1) * HALF]

            def k_half(a, slot, half):
                return a[:, bass.ds(slot, 1), half * HALF:(half + 1) * HALF].rearrange("p a b -> p (a b)")

            def qk_halves(kind, half, head, k_slot):
                if kind == "q":
                    return [half_of(a, head % 2, half) for a in (Q_hi, Q_lo)]
                return [k_half(a, k_slot, half) for a in (K_hi, K_lo)]

            def step(j, i, k_slot, last=False):
                if i == 0 and not last and j in (1, 3):
                    pool.wait_ge(x_done, n["x"])
                    split_wkv()
                for _, _, _, later, _ in ropes_due("add", j, i, last):
                    rope_add(later)
                for kind, half, head, later, _ in ropes_due("low", j, i, last):
                    rope_low(*qk_halves(kind, half, head, k_slot), later)
                if i == 3 and not (last and j >= REP - 2):
                    pool.wait_ge(x_done, n["x"])
                    split_wq()
                if i == 5:
                    if j > 0:
                        pool.wait_ge(y_done, n["y"])
                    split_wo()
                for kind, half, head in finished(j, i, last):
                    if kind in "qk":
                        rope_cos(half)
                    n.add("copy", kind in "qkv")
                    n.add("x")
                n.add("y", j > 0)

            def start(units):
                for kind, half in units:
                    if kind in "qk":
                        rope_cos(half)
                        rope_add()
                        rope_low(*[half_of(a, 0, half) for a in ((Q_hi, Q_lo) if kind == "q" else (K_hi, K_lo))])
                    n.add("copy")
                    n.add("x")

            split_wq()
            split_wkv()
            pool.wait_ge(cos_in, 16)
            start(START[:3])
            pool.wait_ge(x_done, 3)
            split_wkv()
            start(START[3:])
            pool.wait_ge(x_done, 6)
            split_wq()
            for j, i in FIRST_HEAD:
                step(j, i, 0)
            with pool.Fori(0, GROUPS - 1) as g:
                n.enter(g)
                k_slot = pool.snap((g + 1) % 2)
                for j, i in LOOP_STEPS:
                    step(j, i, k_slot)
            n.leave(GROUPS - 1)
            for j, i in LAST_STEPS:
                step(j, i, 0, last=True)

            def act_low(u, unit_no):
                pool.wait_ge(act_hi_done, unit_no)
                half, i2 = divmod(u, 2)
                cols = slice(half * HALF, (half + 1) * HALF)
                nc.gpsimd.tensor_tensor(act[1][:, i2, cols], rope_s[:, u % 2], act[0][:, i2, cols].bitcast(F32),
                                        ALU.subtract).then_inc(act_lo_done, 1)

            with pool.Fori(0, PAIRS) as p:
                for u in range(4):
                    act_low(u, p * 4 + (u + 1))

        @block.scalar
        def _(act_e):
            n = Tally()

            def exponent(j, i):
                slot, at = n.n["tile"] % 2, n.n["tile"] % 4
                act_e.wait_ge(max_done, n["tile"] + 1)
                width = P * (i + 1)
                src, dst = S[:, slot, 0:width], probs[:, slot, 0:width]
                if width > 512:
                    src = S[:, slot].rearrange("p (a b) -> p a b", a=2)[:, :, 0:width // 2]
                    dst = dst.rearrange("p (a b) -> p a b", a=2)
                nc.scalar.activation(dst, src, ACT.Exp, bias=neg_max[:, at:at + 1],
                                     accum_out=row_sum[:, j % 2, i:i + 1]).then_inc(exp_done, 1)
                n.add("tile")

            def tp_high(i):
                for u in range(tp_banks(i)):
                    act_e.wait_ge(tp_done, n["pt"] + 1)
                    dst, src = pt_views(PT_hi, i, u, n.n["pt"] % 2)
                    nc.scalar.activation(dst, src, ACT.Copy).then_inc(tp_hi_done, 1)
                    n.add("pt")

            def rope_high(hi, ago=0):
                act_e.wait_ge(rope_sum_done, n["rope"] - ago)
                nc.scalar.activation(hi, rope_c[:, (n.n["rope"] - 1 - ago) % 2], ACT.Copy).then_inc(rope_hi_done, 1)

            def copy_out(kind, half, bank=0):
                act_e.wait_ge(x_done, n["x"] + 1)
                dst = qk_raw[:, n.n["rope"] % 2] if kind in "qk" else V_stage[:, half * HALF:(half + 1) * HALF]
                if kind in "qk" and n.n["rope"] >= 2:
                    act_e.wait_ge(rope_sum_done, n["rope"] - 1)
                nc.scalar.activation(dst, ACC[:, bank], ACT.Copy).then_inc(copy_done, 1)
                n.add("rope", kind in "qk")
                n.add("x")

            def split_high(kind, half):
                act_e.wait_ge(x_done, n["x"] + 1)
                dst = O_hi[:, half * HALF:(half + 1) * HALF] if kind == "pv" else \
                    V_hi[:, half * HT:(half + 1) * HT, :].rearrange("p a b -> p (a b)")
                nc.scalar.activation(dst, ACC[:, 0], ACT.Copy).then_inc(split_hi_done, 1)
                n.add("x")

            def step(j, i, k_slot, last=False):
                for kind, half, head in finished(j, i, last):
                    if kind in "qkv":
                        copy_out(kind, half)
                    else:
                        split_high(kind, half)
                tp_high(i)
                if not (last and (j, i) == LAST_STEPS[-1]):
                    exponent(j + (i + 1) // NT, (i + 1) % NT)
                for kind, half, head, _, later in ropes_due("high", j, i, last):
                    cols = slice(half * HALF, (half + 1) * HALF)
                    hi = Q_hi[:, head % 2, cols] if kind == "q" else \
                        K_hi[:, bass.ds(k_slot, 1), cols].rearrange("p a b -> p (a b)")
                    rope_high(hi, later)

            def xT_high(half, count, banks, scale=False):
                for c in range(NC):
                    act_e.wait_ge(xt_done, count + c + 1)
                    nc.scalar.activation(xT_hi[:, c, half * HALF:(half + 1) * HALF], banks[c], ACT.Copy,
                                         scale=ln_w_sb[:, c:c + 1] if scale else 1.0).then_inc(xt_hi_done, 1)

            xT_high(0, 0, xbank[1])
            xT_high(1, NC, xbank[0])
            for u, (kind, half) in enumerate(START):
                copy_out(kind, half, u % 2)
                if kind in "qk":
                    rope_high((Q_hi if kind == "q" else K_hi)[:, 0, half * HALF:(half + 1) * HALF])
            exponent(0, 0)
            for j, i in FIRST_HEAD:
                step(j, i, 0)
            with act_e.Fori(0, GROUPS - 1) as g:
                n.enter(g)
                k_slot = act_e.snap((g + 1) % 2)
                for j, i in LOOP_STEPS:
                    step(j, i, k_slot)
            n.leave(GROUPS - 1)
            for j, i in LAST_STEPS:
                step(j, i, 0, last=True)
            split_high("pv", 1)

            def deviation(cols, squares, eps, scale):
                nc.scalar.activation(spread[:, cols], squares, ACT.Sqrt, bias=eps[:], scale=scale).then_inc(std_done, 1)

            def layer_deviation(half):
                act_e.wait_ge(var_done, (half + 1) * HT)
                cols = slice(half * HT, (half + 1) * HT)
                deviation(cols, mean_var[:, cols, 1], eps_ln, 1.0)

            def rms_deviation(half):
                for t in range(half * HT, (half + 1) * HT):
                    act_e.wait_ge(ln_done, t + 1)
                    if t >= 2:
                        act_e.wait_ge(sq_done, t - 1)
                    nc.scalar.activation(V_stage[:, t % 2 * HID:(t % 2 + 1) * HID], y[:, t, :], ACT.Square,
                                         accum_out=sum_sq[:, t:t + 1]).then_inc(sq_done, 1)
                act_e.wait_ge(sq_done, (half + 1) * HT)
                cols = slice(half * HT, (half + 1) * HT)
                deviation(cols, sum_sq[:, cols], eps_rms, 1.0 / HID)

            tp_base = HEADS * 12

            def weight_high(dst, v, parity):
                act_e.wait_ge(tp_done, v + 1)
                nc.scalar.activation(dst, TP[:, parity].rearrange("p (a b) -> p a b", b=P), ACT.Copy).then_inc(tp_hi_done, 1)

            def gate_up_high(k, v0):
                weight_high((gT, uT)[k // 2][0][:, :, k % 2 * P:(k % 2 + 1) * P], v0 + k, k % 2)

            def down_high(i2, v0):
                weight_high(dT[0][:, i2].rearrange("p (a b) -> p a b", b=P), v0 + i2, i2)

            def activation(p, u):
                half, i2 = divmod(u, 2)
                act_e.wait_ge(gu_done, p * 4 + (u + 1))
                nc.scalar.activation(rope_c[:, u % 2], S[:, u % 2, 0:HALF], ACT.Silu).then_inc(silu_done, 1)
                act_e.wait_ge(prod_done, p * 4 + (u + 1))
                nc.scalar.activation(act[0][:, i2, half * HALF:(half + 1) * HALF], rope_s[:, u % 2], ACT.Copy).then_inc(act_hi_done, 1)

            def pair(p, last=False):
                for u in range(4):
                    activation(p, u)
                    if u in (1, 2):
                        down_high(u - 1, p * 6 + (tp_base + 4))
                for k in range(0 if last else 4):
                    gate_up_high(k, p * 6 + (tp_base + 6))

            act_e.wait_ge(eps_done, 1)
            layer_deviation(0)
            gate_up_high(0, tp_base)
            gate_up_high(1, tp_base)
            rms_deviation(0)
            gate_up_high(2, tp_base)
            gate_up_high(3, tp_base)
            xT_high(0, 2 * NC, xbank[0], scale=True)
            layer_deviation(1)
            rms_deviation(1)
            activation(0, 0)
            xT_high(1, 3 * NC, xbank[1], scale=True)
            for u in range(1, 4):
                activation(0, u)
                if u < 3:
                    down_high(u - 1, tp_base + 4)
            for k in range(4):
                gate_up_high(k, tp_base + 6)
            with act_e.Fori(1, PAIRS - 1) as p:
                pair(p)
            pair(PAIRS - 1, last=True)

            for t in range(NT):
                act_e.wait_ge(var_done, NT + t + 1)
                deviation(slice(t, t + 1), mean_var[:, t, 1:2], eps_ln, 1.0)

        @block.vector
        def _(dve):
            n = Tally()

            def maximum(i):
                slot, at = n.n["tile"] % 2, n.n["tile"] % 4
                dve.wait_ge(score_done, n["tile"] + 1)
                width = P * (i + 1)
                src = S[:, slot, 0:width]
                if width > 512:
                    src = S[:, slot].rearrange("p (a b) -> p a b", a=2)[:, :, 0:width // 2]
                if n.n["tile"] >= 4:
                    dve.wait_ge(exp_done, n["tile"] - 3)
                nc.vector.tensor_reduce(neg_max[:, at:at + 1], src, AX.XY if width > 512 else AX.X, ALU.max,
                                        negate=True).then_inc(max_done, 1)
                n.add("tile")

            def tp_low(i):
                for u in range(tp_banks(i)):
                    dve.wait_ge(tp_hi_done, n["pt"] + 1)
                    hi, src = pt_views(PT_hi, i, u, n.n["pt"] % 2)
                    lo, _ = pt_views(PT_lo, i, u, n.n["pt"] % 2)
                    nc.vector.tensor_tensor(lo, src, hi.bitcast(F32), ALU.subtract).then_inc(tp_lo_done, 1)
                    n.add("pt")

            def rope_sin(part, half, ago=0):
                r, cols, h = (n.n["rope"] - 1 - ago) % 2, slice(half * HALF, (half + 1) * HALF), HD // 2
                src, dst = (slice(h, P), slice(0, h)) if part == 0 else (slice(0, h), slice(h, P))
                if part == 0:
                    dve.wait_ge(copy_done, n["copy"])
                nc.vector.tensor_tensor(rope_s[dst, r], qk_raw[src, r], sin_sb[src, cols], ALU.mult).then_inc(rope_s_done, 1)

            def copied(kind):
                n.add("copy")
                n.add("rope", kind in "qk")

            def split_low(kind, half, head):
                dve.wait_ge(split_hi_done, n["split"] + 1)
                hi, lo = [a[:, half * HALF:(half + 1) * HALF] for a in (O_hi, O_lo)] if kind == "pv" else \
                    [a[:, half * HT:(half + 1) * HT, :].rearrange("p a b -> p (a b)") for a in (V_hi, V_lo)]
                nc.vector.tensor_tensor(lo, ACC[:, 0], hi.bitcast(F32), ALU.subtract).then_inc(split_done, 1)
                n.add("split")
                if kind == "pv":
                    reciprocals(head, half)

            def reciprocals(head, half):
                rows = slice(half * HT, (half + 1) * HT)
                nc.vector.reciprocal(row_rcp[:, head % 2, rows], row_sum[:, head % 2, rows]).then_inc(rcp_done, 1)
                n.add("recip")

            def add_rows(t, head, tail=False):
                dve.wait_ge(y_done, n["y"] + 1)
                dve.wait_ge(rcp_done, n["recip"])
                nc.vector.scalar_tensor_tensor(out=y[:, t, :], in0=ACC[:, y_bank(t, tail)],
                                               scalar=row_rcp[:, head % 2, t:t + 1], in1=y[:, t, :],
                                               op0=ALU.mult, op1=ALU.add).then_inc(y_free, 1)
                n.add("y")

            def step(j, i, last=False):
                if not (last and (j, i) == LAST_STEPS[-1]):
                    maximum((i + 1) % NT)
                for kind, half, head in finished(j, i, last):
                    if kind in "qkv":
                        copied(kind)
                    else:
                        split_low(kind, half, head)
                tp_low(i)
                if j > 0:
                    add_rows(i, j - 1)
                for part in range(2):
                    for _, half, _, _, later in ropes_due(f"sin{part}", j, i, last):
                        rope_sin(part, half, later)

            nc.vector.memset(eps_ln[:], LN_EPS).then_inc(eps_done, 1)
            for half in range(2):
                for c in range(NC):
                    dve.wait_ge(xt_hi_done, half * NC + c + 1)
                    cols = slice(half * HALF, (half + 1) * HALF)
                    nc.vector.tensor_tensor(xT_lo[:, c, cols], xbank[1 - half][c], xT_hi[:, c, cols].bitcast(F32), ALU.subtract).then_inc(xt_lo_done, 1)
            dve.wait_ge(sin_in, 16)
            for kind, half in START:
                copied(kind)
                if kind in "qk":
                    rope_sin(0, half)
                    rope_sin(1, half)
            nc.vector.memset(eps_rms[:], RMS_EPS).then_inc(y_free, 1)
            maximum(0)
            for j, i in FIRST_HEAD:
                step(j, i)
            with dve.Fori(0, GROUPS - 1) as g:
                n.enter(g)
                for j, i in LOOP_STEPS:
                    step(j, i)
            n.leave(GROUPS - 1)
            for j, i in LAST_STEPS:
                step(j, i, last=True)
            tp_base = HEADS * 12

            def weight_low(w, v, parity):
                hi, lo = w
                dve.wait_ge(tp_hi_done, v + 1)
                nc.vector.tensor_tensor(lo, TP[:, parity].rearrange("p (a b) -> p a b", b=P), hi.bitcast(F32),
                                        ALU.subtract).then_inc(tp_lo_done, 1)

            def gate_up_low(k, v0):
                weight_low([a[:, :, k % 2 * P:(k % 2 + 1) * P] for a in (gT, uT)[k // 2]], v0 + k, k % 2)

            def down_low(i2, v0):
                weight_low([a[:, i2].rearrange("p (a b) -> p a b", b=P) for a in dT], v0 + i2, i2)

            def product(p, u, first=False):
                dve.wait_ge(silu_done, p * 4 + (u + 1))
                if u >= 2 or not first:
                    dve.wait_ge(act_lo_done, p * 4 + (u - 1))
                nc.vector.tensor_tensor(rope_s[:, u % 2], S[:, u % 2, HALF:2 * HALF], rope_c[:, u % 2],
                                        ALU.mult).then_inc(prod_done, 1)

            def down_add(p, t):
                dve.wait_ge(y_done, p * NT + (y_base + t + 1))
                nc.vector.tensor_tensor(y[:, t, :], ACC[:, t % 2], y[:, t, :], ALU.add).then_inc(y_free, 1)

            def pair(p):
                for u in range(4):
                    product(p, u)
                    if u in (1, 2):
                        down_low(u - 1, p * 6 + (tp_base + 4))
                for t in range(NT):
                    down_add(p, t)
                    if t < 4:
                        gate_up_low(t, p * 6 + (tp_base + 6))

            def variances(t, rows_done):
                dve.wait_ge(y_free, rows_done + 1)
                nc.vector.bn_stats(stats[:, t, :], y[:, t, :]).then_inc(stats_done, 1)
                n.add("stats")
                dve.wait_ge(stats_done, n["stats"])
                nc.vector.bn_aggr(mean_var[:, t, :], stats[:, t, :]).then_inc(var_done, 1)

            def inverses(turn, cols):
                dve.wait_ge(std_done, turn)
                nc.vector.reciprocal(inv_spread[:, cols], spread[:, cols]).then_inc(inv_done, 1)
                dve.wait_ge(inv_done, turn)

            def layer_norm(t):
                return nc.vector.tensor_scalar(y[:, t, :], y[:, t, :], mean_var[:, t, 0:1], inv_spread[:, t:t + 1],
                                               ALU.subtract, ALU.mult)

            def rms_norm(t):
                nc.vector.tensor_scalar(nx[t], y[:, t, :], inv_spread[:, t:t + 1], None, ALU.mult).then_inc(nx_done, 1)

            def xT_low(half):
                for c in range(NC):
                    dve.wait_ge(xt_hi_done, (2 + half) * NC + c + 1)
                    cols = slice(half * HALF, (half + 1) * HALF)
                    nc.vector.scalar_tensor_tensor(out=xT_lo[:, c, cols], in0=xbank[half][c], scalar=ln_w_sb[:, c:c + 1],
                                                   in1=xT_hi[:, c, cols].bitcast(F32), op0=ALU.mult,
                                                   op1=ALU.subtract).then_inc(xt_lo_done, 1)

            tiles = [range(HT), range(HT, NT)]
            cols = [slice(0, HT), slice(HT, NT)]
            dve.wait_ge(ln_w_in, 16)
            add_rows(0, REP - 1, tail=True)
            split_low("pv", 1, REP - 1)
            for t in range(1, HT):
                add_rows(t, REP - 1, tail=True)
            for t in tiles[0]:
                variances(t, n["y"])
            inverses(1, cols[0])
            for t in tiles[0]:
                layer_norm(t).then_inc(ln_done, 1)
            gate_up_low(0, tp_base)
            gate_up_low(1, tp_base)
            for t in (4, 5):
                add_rows(t, REP - 1, tail=True)
            inverses(2, cols[0])
            for t in tiles[0]:
                rms_norm(t)
            gate_up_low(2, tp_base)
            gate_up_low(3, tp_base)
            for t in (6, 7):
                add_rows(t, REP - 1, tail=True)
            y_base = n["y"]
            xT_low(0)
            for t in tiles[1]:
                variances(t, y_base)
            inverses(3, cols[1])
            for t in tiles[1]:
                layer_norm(t).then_inc(ln_done, 1)
            inverses(4, cols[1])
            for t in tiles[1]:
                rms_norm(t)
            product(0, 0, first=True)
            xT_low(1)

            for u in range(1, 4):
                product(0, u, first=True)
                if u < 3:
                    down_low(u - 1, tp_base + 4)
            for t in range(NT):
                down_add(0, t)
                if t < 4:
                    gate_up_low(t, tp_base + 6)
            with dve.Fori(1, PAIRS - 1) as p:
                pair(p)
            for u in range(4):
                product(PAIRS - 1, u)
                if u in (1, 2):
                    down_low(u - 1, (PAIRS - 1) * 6 + (tp_base + 4))

            def finish(t):
                inverses(5 + t, slice(t, t + 1))
                layer_norm(t).then_inc(out_ready, 1)

            for t in range(NT):
                down_add(PAIRS - 1, t)
                variances(t, y_base + (PAIRS - 1) * NT + t + 1)
                if t >= 1:
                    finish(t - 1)
            finish(NT - 1)

        @block.tensor
        def _(pe):
            n = Tally()

            def product(dst, a, b, start, stop):
                nc.tensor.matmul(dst, a[0], b[0], start=start, stop=False)
                nc.tensor.matmul(dst, a[0], b[1], start=False, stop=False)
                return nc.tensor.matmul(dst, a[1], b[0], start=False, stop=stop)

            def scores(j, i, k_slot):
                slot = n.n["tile"] % 2
                if i % HT == 0:
                    pe.wait_ge(rope_lo_done, n.marked(("q", i // HT, j % 2)))
                if n.n["tile"] >= 2:
                    pe.wait_ge(exp_done, n["tile"] - 1)
                q = [a[:, j % 2, i * P:(i + 1) * P] for a in (Q_hi, Q_lo)]
                for col, key, width in score_chunks(i):
                    dst = S[:, slot, col:col + width]
                    k = [a[:, bass.ds(k_slot, 1), key:key + width].rearrange("p a b -> p (a b)") for a in (K_hi, K_lo)]
                    nc.tensor.matmul(dst, q[0], k[0], start=True, stop=False)
                    if key + width == P * (i + 1):
                        nc.tensor.matmul(S[:, slot, col + width - P:col + width], ident_bf[:], mask_bf[:],
                                         start=False, stop=False)
                    nc.tensor.matmul(dst, q[0], k[1], start=False, stop=False)
                    last = nc.tensor.matmul(dst, q[1], k[0], start=False, stop=True)
                last.then_inc(score_done, 1)
                n.add("tile")

            def transposes(i, tile):
                pe.wait_ge(exp_done, n.at("tile", tile + 1))
                for u in range(tp_banks(i)):
                    bank = n.n["pt"] % 2
                    if n.n["pt"] >= 2:
                        pe.wait_ge(tp_lo_done, n["pt"] - 1)
                    for b in range(4 * u, min(4 * u + 4, i + 1)):
                        last = nc.tensor.transpose(TP[:, bank, (b % 4) * P:(b % 4 + 1) * P],
                                                   probs[:, tile % 2, b * P:(b + 1) * P], ident[:])
                    last.then_inc(tp_done, 1)
                    n.add("pt")
                n.mark(("pt", i), "pt")

            def other(kind, half, head, begin, end, bank=0):
                acc, count = ACC[:, bank], products(kind, half)
                if begin == 0 and ("bank", bank) in n.marks:
                    pe.wait_ge(copy_done if n.marks["bank", bank][0] == "copy" else split_done, n.marked(("bank", bank)))
                if begin == 0 and kind in "qkv":
                    if kind == "q":
                        pe.wait_ge(wq_done, n["wq"] + 1)
                    else:
                        pe.wait_ge(wkv_done, n["wkv"] + 1)
                if begin == 0 and kind == "pv":
                    pe.wait_ge(tp_lo_done, n.marked(("pt", HT * (half + 1) - 1)))
                for k in range(begin, end):
                    if kind in "qkv":
                        w = (wq_hi, wq_lo) if kind == "q" else (wkv_hi, wkv_lo)
                        cols = slice(half * HALF, (half + 1) * HALF)
                        last = product(acc, [a[:, k, :] for a in w], [a[:, k, cols] for a in (xT_hi, xT_lo)],
                                       k == 0, k == count - 1)
                    if kind == "vt":
                        key = (half * HT + k) * P
                        last = nc.tensor.transpose(acc[:, k * P:(k + 1) * P], V_stage[:, key:key + P], ident[:])
                    if kind == "pv":
                        skip = max(0, k - HT * half) * P
                        row = HT * half + k
                        last = product(acc[:, skip:HALF], [v[:, k, :] for v in (V_hi, V_lo)],
                                       [p[:, row, skip:HALF] for p in (PT_hi, PT_lo)], k == 0, k == count - 1)
                if end < count:
                    return
                last.then_inc(x_done, 1)
                released = "copy" if kind in "qkv" else "split"
                n.add(released)
                n.mark(("bank", bank), released)
                if kind == "pv":
                    n.mark((kind, half), released)
                if kind in "qk":
                    n.add("rope")
                    n.mark((kind, half, head % 2), "rope")
                if half == 1 and kind in "qkv":
                    n.add("wq" if kind == "q" else "wkv")

            def rows(t, tail=False):
                if t % HT == 0:
                    pe.wait_ge(split_done, n.marked(("pv", t // HT)))
                pe.wait_ge(wo_done, n["wo"] + 1)
                bank = y_bank(t, tail)
                if tail and t == 2:
                    pe.wait_ge(split_done, n.marked(("pv", 1)))
                else:
                    pe.wait_ge(y_free, n["y"] + (0 if tail and t > 2 else 1))
                cols, slot = slice(t * P, (t + 1) * P), n.n["wo"] % 2
                product(ACC[:, bank], (O_hi[:, cols], O_lo[:, cols]), (wo_hi[:, slot], wo_lo[:, slot]), True, True).then_inc(y_done, 1)
                n.add("y")
                n.add("wo", t == NT - 1)

            def step(j, i, slots, last=False):
                tile = n.n["tile"] - 1
                if not (last and (j, i) == LAST_STEPS[-1]):
                    following = j + (i + 1) // NT
                    scores(following, (i + 1) % NT, slots[following // REP])
                for part in extras(j, i, last):
                    other(*part)
                transposes(i, tile)
                if j > 0:
                    rows(i)

            def transpose_rows(src, half, banks):
                for c in range(NC):
                    for t in range(HT):
                        last = nc.tensor.transpose(banks[c][:, t * P:(t + 1) * P],
                                                   src(half * HT + t)[:, c * P:(c + 1) * P], ident[:])
                    last.then_inc(xt_done, 1)

            pe.wait_ge(const_done, 7)
            for half in range(2):
                pe.wait_ge(x_in[half], 16)
                transpose_rows(lambda t: y[:, t, :], half, xbank[1 - half])
            pe.wait_ge(xt_lo_done, NC)
            for u, (kind, half) in enumerate(START):
                if u == 2:
                    n.mark(("q", 0, 0), "rope")
                    pe.wait_ge(xt_lo_done, 2 * NC)
                other(kind, half, 0, 0, NC, bank=u % 2)
            scores(0, 0, 0)
            for j, i in FIRST_HEAD:
                step(j, i, (0, 0))
            with pe.Fori(0, GROUPS - 1) as g:
                n.enter(g)
                slots = (pe.snap(g % 2), pe.snap((g + 1) % 2))
                for j, i in LOOP_STEPS:
                    step(j, i, slots)
            n.leave(GROUPS - 1)
            for j, i in LAST_STEPS:
                step(j, i, ((GROUPS - 1) % 2, 0), last=True)

            tp_base = HEADS * 12

            def weight_transposes(bank, blocks, v):
                pe.wait_ge(tp_lo_done, v - 1)
                for b, block in enumerate(blocks):
                    last = nc.tensor.transpose(TP[:, bank, b * P:(b + 1) * P], block, ident[:])
                last.then_inc(tp_done, 1)

            def gate_up_transposes(p, k, v0):
                if k == 0:
                    pe.wait_ge(gate_in, p * 16 + 16)
                if k == 2:
                    pe.wait_ge(up_in, p * 16 + 16)
                raw = (gate_raw, up_raw)[k // 2]
                weight_transposes(k % 2, [raw[:, k % 2, c * P:(c + 1) * P] for c in range(NC)], v0 + k)

            def down_transposes(p, i2, v0):
                pe.wait_ge(down_in, p * 16 + 16)
                weight_transposes(i2, [down_raw[:, c, i2 * P:(i2 + 1) * P] for c in range(NC)], v0 + i2)

            def gate_up(p, u, first=False):
                half, i2 = divmod(u, 2)
                if u >= 2 or not first:
                    pe.wait_ge(prod_done, p * 4 + (u - 1))
                cols, rows = slice(half * HALF, (half + 1) * HALF), slice(i2 * P, (i2 + 1) * P)
                for bank, w in enumerate((gT, uT)):
                    for c in range(NC):
                        last = product(S[:, u % 2, bank * HALF:(bank + 1) * HALF], [a[:, c, rows] for a in w],
                                       [a[:, c, cols] for a in (xT_hi, xT_lo)], c == 0, c == NC - 1)
                last.then_inc(gu_done, 1)

            def down(p, t):
                if t % HT == 0:
                    pe.wait_ge(act_lo_done, p * 4 + (2 + t // HT * 2))
                pe.wait_ge(y_free, p * NT + (y_base + t))
                cols = slice(t * P, (t + 1) * P)
                for i2 in range(2):
                    last = product(ACC[:, t % 2], [a[:, i2, cols] for a in act], [a[:, i2, :] for a in dT],
                                   i2 == 0, i2 == 1)
                last.then_inc(y_done, 1)

            def downs(p, last=False):
                pe.wait_ge(tp_lo_done, p * 6 + (tp_base + 6))
                for t in range(NT):
                    down(p, t)
                    if t < 4 and not last:
                        gate_up_transposes(p + 1, t, p * 6 + (tp_base + 6))

            def pair(p, last=False):
                pe.wait_ge(tp_lo_done, p * 6 + (tp_base + 4))
                for u in range(4):
                    gate_up(p, u)
                    if u in (1, 2):
                        down_transposes(p, u - 1, p * 6 + (tp_base + 4))
                downs(p, last)

            rows(0, tail=True)
            other("pv", 1, REP - 1, 0, NT)
            for t in range(1, HT):
                rows(t, tail=True)
            gate_up_transposes(0, 0, tp_base)
            gate_up_transposes(0, 1, tp_base)
            for t in (4, 5):
                rows(t, tail=True)
            gate_up_transposes(0, 2, tp_base)
            gate_up_transposes(0, 3, tp_base)
            for t in (6, 7):
                rows(t, tail=True)
            y_base = n["y"]
            pe.wait_ge(nx_done, HT)
            transpose_rows(lambda t: nx[t], 0, xbank[0])
            pe.wait_ge(xt_lo_done, 3 * NC)
            pe.wait_ge(tp_lo_done, tp_base + 4)
            gate_up(0, 0, first=True)
            pe.wait_ge(nx_done, NT)
            pe.wait_ge(y_free, y_base + 1)
            transpose_rows(lambda t: nx[t], 1, xbank[1])
            gate_up(0, 1, first=True)
            pe.wait_ge(xt_lo_done, 4 * NC)
            down_transposes(0, 0, tp_base + 4)
            gate_up(0, 2, first=True)
            down_transposes(0, 1, tp_base + 4)
            gate_up(0, 3, first=True)
            downs(0)
            with pe.Fori(1, PAIRS - 1) as p:
                pair(p)
            pair(PAIRS - 1, last=True)


def rope_tables():
    import numpy as np
    theta, factor, hi_ff, lo_ff, orig_max = 500000.0, 8.0, 4.0, 1.0, 1024
    inv = 1.0 / theta ** (np.arange(0, HD, 2, dtype=np.float64) / HD)
    wavelen = 2.0 * np.pi / inv
    low_wl, high_wl = orig_max / lo_ff, orig_max / hi_ff
    smooth = (orig_max / wavelen - lo_ff) / (hi_ff - lo_ff)
    scaled = np.where(wavelen > low_wl, inv / factor, inv)
    mid = (wavelen <= low_wl) & (wavelen >= high_wl)
    scaled = np.where(mid, (1 - smooth) * inv / factor + smooth * inv, scaled).astype(np.float32)
    freqs = np.arange(T, dtype=np.float32)[None, :] * scaled[:, None]
    scale = float(HD) ** -0.25
    cos = np.cos(freqs).astype(np.float64) * scale
    sin = np.sin(freqs).astype(np.float64) * scale
    return (np.concatenate([cos, cos]).astype(np.float32), np.concatenate([sin, -sin]).astype(np.float32))


_INS = ['L0_attn_x', 'L0_attn_wq', 'L0_attn_wk', 'L0_attn_wv', 'L0_attn_wo',
        'L0_ffn_ln_w', 'L0_ffn_gate_w', 'L0_ffn_up_w', 'L0_ffn_down_w']


def kernel(**inputs):
    import numpy as np
    import concourse.bacc as bacc
    from concourse.bass_utils import run_bass_kernel_spmd

    nc = bacc.Bacc("TRN2", target_bir_lowering=False, num_devices=1)
    arrays, args = {}, []
    for name in _INS:
        arrays[f"in_{name}_dram"] = np.ascontiguousarray(inputs[name])
    for name, table in zip(("cos", "sin"), rope_tables()):
        arrays[f"in_{name}_dram"] = table
    for name, a in arrays.items():
        args.append(nc.dram_tensor(name, a.shape, mybir.dt.from_np(a.dtype), kind="ExternalInput").ap())
    args.append(nc.dram_tensor("out_0_dram", (1, T, HID), F32, kind="ExternalOutput").ap())
    layer_kernel(nc, *args)
    r = run_bass_kernel_spmd(nc, [arrays], core_ids=[0])
    return r.results[0]["out_0_dram"]
```

```python
from contextlib import ExitStack

import concourse.bass as bass
from concourse import mybir

F32 = mybir.dt.float32
F32R = mybir.dt.float32r
ALU = mybir.AluOpType
ACT = mybir.ActivationFunctionType
AX = mybir.AxisListType

P = 128
HEADS, KV_HEADS, HD = 32, 8, 128
T, HID, INTER = 1024, 512, 1792
REP = HEADS // KV_HEADS
NT = T // P
NC = HID // P
HALF = T // 2
HT = NT // 2
GROUPS = KV_HEADS
PAIRS = INTER // (2 * P)
LN_EPS = 1e-5
RMS_EPS = 1e-5
SCALAR_TILES = NT - 1
EARLY_TILES = 2
WARM_UP = 9
MASKED = -3.0e38


class Tally:

    PER = {
        "tile": REP * NT,
        "pt": REP * 12,
        "x": REP * 4 + 6,
        "copy": REP * 2 + 4,
        "split": REP * 2 + 2,
        "y": REP * NT,
        "rope": REP * 2 + 2,
        "rot0": REP + 1, "rot1": REP + 1,
        "product": REP * 4 + 4,
        "recip": REP * 2,
        "wq": REP, "wo": REP, "wkv": 2,
        "stats": 0,
    }

    def __init__(self):
        self.n = dict.fromkeys(self.PER, 0)
        self.marks = {}
        self.group = 0

    def __getitem__(self, kind):
        return self.n[kind] + self.PER[kind] * self.group

    def at(self, kind, local):
        return local + self.PER[kind] * self.group

    def mark(self, name, kind):
        self.marks[name] = (kind, self.n[kind])

    def marked(self, name):
        return self.at(*self.marks[name])

    def add(self, kind, count=1):
        self.n[kind] += count

    def enter(self, group):
        self.group = group

    def leave(self, iterations):
        self.group = 0
        for kind, per in self.PER.items():
            self.n[kind] += per * (iterations - 1)
        for name, (kind, local) in self.marks.items():
            self.marks[name] = (kind, local + self.PER[kind] * (iterations - 1))


def products(kind, half):
    return {"pv": HT * (half + 1), "vt": HT}.get(kind, NC)


def extras(j, i, last=False):
    heads = REP if last else 2 * REP
    if j == 0 and i in (0, 1):
        return [("q", i, 1, 0, NC)]
    if i == 0 and j + 1 < heads:
        return [("q", 1, j + 1, 0, NC)]
    if i == 7 and j + 2 < heads:
        return [("q", 0, j + 2, 0, NC)]
    if last and i in (1, 2, 3):
        return [("pv", 1, j - 1, 3 * i - 3, min(3 * i, NT))]
    if last and i in (4, 5, 6):
        return [("pv", 0, j, i - 4, HT if i == 6 else i - 3)]
    if i in (1, 2) and j > 0:
        return [("pv", 1, j - 1, (i - 1) * HT, i * HT)]
    if i in (3, 4) and j % REP == 0:
        return [("vt", i - 3, j, 0, HT)]
    if i in (3, 4) and j < REP - 1 and not last:
        return [("k", j - 1, REP, (i - 3) * NC // 2, (i - 2) * NC // 2)]
    if i in (3, 4) and not last:
        return [("v", i - 3, REP, 0, NC)]
    if i == 5:
        return [("pv", 0, j, 0, 1)]
    if i == 6:
        return [("pv", 0, j, 1, HT)]
    return []


def finished(j, i, last=False):
    return [(kind, half, head) for kind, half, head, _, end in extras(j, i, last) if end == products(kind, half)]


ROPE_STEPS = {"sum": 1, "high": 2, "low": 3}
FIRST_STEPS = {"sum": 1, "high": 3, "low": 4}


def ropes_due(stage, j, i, last=False):
    def projected(ago):
        jj, ii = divmod(j * NT + i - ago, NT)
        return [unit for unit in (finished(jj, ii, last) if jj >= 0 else []) if unit[0] in "qk"]

    due = []
    for ago in range(1, max(FIRST_STEPS.values()) + 1):
        first = (j * NT + i - ago) < HT and not last
        if ago == (FIRST_STEPS if first else ROPE_STEPS)[stage]:
            before = sum(len(projected(later)) for later in range(1, ago))
            due += [unit + (before, before + len(projected(0))) for unit in projected(ago)]
    return due


FIRST_HEAD = [(0, i) for i in range(NT)]
LOOP_STEPS = [(j, i) for j in range(1, REP + 1) for i in range(NT)]
LAST_STEPS = [(j, i) for j in range(1, REP) for i in range(NT)]
X_PARTS = [(0, 0, 1), (0, 1, 2), (0, 2, NC), (1, 0, 2), (1, 2, NC)]
START = [("q", 0), ("k", 0), ("q", 1), ("k", 1), ("v", 0), ("v", 1)]


def y_bank(t, tail=False):
    return (t if t < HT else t + 1) % 2 if tail else 1


def tp_banks(i):
    return i // 4 + 1


def score_chunks(i):
    width = P * (i + 1)
    if width <= 512:
        return [(0, 0, width)]
    return [(0, 0, width // 2), (512, width // 2, width // 2)]


def layer_kernel(nc, x, x_t, wq, wk, wv, wo, ln_w, gate_t, up_t, down_t, cos_t, sin_t, out):
    x_v = x.rearrange("b (i p) d -> p (b i) d", p=P)
    out_v = out.rearrange("b (i p) d -> p (b i) d", p=P)
    wq_v = wq.rearrange("(c p) n -> p c n", p=P)
    wk_v = wk.rearrange("(c p) n -> p c n", p=P)
    wv_v = wv.rearrange("(c p) n -> p c n", p=P)
    ln_w_v = ln_w.rearrange("(c p) -> p c", p=P)
    x_t_v = x_t.rearrange("(c p) t -> p c t", p=P)
    gate_v = gate_t.rearrange("(c p) i -> p c i", p=P)
    up_v = up_t.rearrange("(c p) i -> p c i", p=P)
    down_v = down_t.rearrange("(n p) k -> p n k", p=P)

    with ExitStack() as ctx:
        def sb(name, shape, dt=F32):
            return ctx.enter_context(nc.sbuf_tensor(name, [P] + shape, dt))

        def sem(name):
            return ctx.enter_context(nc.semaphore(name))

        y = sb("y", [NT, HID])
        xT_hi, xT_lo = sb("xT_hi", [NC, T], F32R), sb("xT_lo", [NC, T], F32R)
        PT_hi, PT_lo = sb("PT_hi", [12, HALF], F32R), sb("PT_lo", [12, HALF], F32R)
        Q_hi, Q_lo = sb("Q_hi", [2, T], F32R), sb("Q_lo", [2, T], F32R)
        K_hi, K_lo = sb("K_hi", [2, T], F32R), sb("K_lo", [2, T], F32R)
        V_hi, V_lo = sb("V_hi", [NT, HD], F32R), sb("V_lo", [NT, HD], F32R)
        O_hi, O_lo = sb("O_hi", [T], F32R), sb("O_lo", [T], F32R)
        V_stage = sb("V_stage", [T])
        cos_sb, sin_sb = sb("cos_sb", [T]), sb("sin_sb", [T])
        wq_raw, wq_hi, wq_lo = sb("wq_raw", [NC, HD]), sb("wq_hi", [NC, HD], F32R), sb("wq_lo", [NC, HD], F32R)
        wkv_raw, wkv_hi, wkv_lo = sb("wkv_raw", [NC, HD]), sb("wkv_hi", [NC, HD], F32R), sb("wkv_lo", [NC, HD], F32R)
        wo_raw, wo_hi, wo_lo = sb("wo_raw", [HID]), sb("wo_hi", [2, HID], F32R), sb("wo_lo", [2, HID], F32R)
        probs = sb("probs", [2, T])
        qk_raw, rope_c, rope_s = sb("qk_raw", [2, HALF]), sb("rope_c", [2, HALF]), sb("rope_s", [2, HALF])
        gate_raw, up_raw = sb("gate_raw", [NC, 2 * P]), sb("up_raw", [NC, 2 * P])
        ident, mask = sb("ident", [P]), sb("mask", [P])
        neg_max = sb("neg_max", [4])
        row_sum, row_rcp = sb("row_sum", [2, NT]), sb("row_rcp", [2, NT])
        ln_w_sb = sb("ln_w_sb", [NC])
        stats, mean_var, sum_sq = sb("stats", [NT, 6]), sb("mean_var", [NT, 2]), sb("sum_sq", [NT])
        shift = sb("shift", [NT])
        spread, inv_spread = sb("spread", [NT]), sb("inv_spread", [NT])
        zero = sb("zero", [1])
        eps_ln, eps_rms = sb("eps_ln", [1]), sb("eps_rms", [1])
        table_scratch = sb("table_scratch", [1])

        def part(tensor, at, shape):
            size = shape[0] * shape[1]
            flat = tensor[:].rearrange("p a b -> p (a b)")[:, at:at + size]
            return flat.rearrange("p (a b) -> p a b", b=shape[1])

        gT = [part(t, 0, (NC, 2 * P)) for t in (PT_hi, PT_lo)]
        uT = [part(t, NC * 2 * P, (NC, 2 * P)) for t in (PT_hi, PT_lo)]
        dT = [part(t, NC * 4 * P, (2, HID)) for t in (PT_hi, PT_lo)]
        act = [part(t, NC * 4 * P + 2 * HID, (2, T)) for t in (PT_hi, PT_lo)]
        nx = [b[:, k * HID:(k + 1) * HID] for b in (cos_sb, sin_sb) for k in range(2)]
        nx += [qk_raw[:, 0], qk_raw[:, 1]] + [w[:].rearrange("p a b -> p (a b)") for w in (wq_raw, wkv_raw)]
        down_raw = part(probs, 0, (2, HID))
        xT_raw = part(y, 0, (NC, T))

        S = ctx.enter_context(nc.psum_tensor("S", [P, 2, T], F32))
        TP = ctx.enter_context(nc.psum_tensor("TP", [P, 2, HALF], F32))
        ACC = ctx.enter_context(nc.psum_tensor("ACC", [P, 2, HALF], F32))
        xbank = [[S[:, c // 2, (c % 2) * HALF:(c % 2 + 1) * HALF] for c in range(NC)],
                 [TP[:, 0], TP[:, 1], ACC[:, 0], ACC[:, 1]]]

        def pt_views(dst, i, u, bank):
            blocks = min(4, i + 1 - 4 * u)
            row = (0 if i < HT else HT) + 4 * u
            col = (i % HT) * P
            return dst[:, row:row + blocks, col:col + P], TP[:, bank, 0:blocks * P].rearrange("p (a b) -> p a b", b=P)

        x_in, x_t_in = sem("x_in"), [sem(f"x_t_in{part}") for part in range(len(X_PARTS))]
        cos_in, sin_in, ln_w_in = sem("cos_in"), sem("sin_in"), sem("ln_w_in")
        wq_in, wkv_in, wo_in = sem("wq_in"), sem("wkv_in"), sem("wo_in")
        gate_in, up_in, down_in = sem("gate_in"), sem("up_in"), sem("down_in")
        const_done = sem("const_done")
        w_hi_done = sem("w_hi_done")
        wq_done, wkv_done, wo_done = sem("wq_done"), sem("wkv_done"), sem("wo_done")
        fw_hi_done, fw_lo_done = sem("fw_hi_done"), sem("fw_lo_done")
        xt_done, xt_hi_done, xt_lo_done = sem("xt_done"), sem("xt_hi_done"), sem("xt_lo_done")
        score_done = sem("score_done")
        mask_done = sem("mask_done")
        max_done = sem("max_done")
        exp_done = sem("exp_done")
        tp_done = sem("tp_done")
        tp_hi_done = sem("tp_hi_done")
        tp_lo_done = sem("tp_lo_done")
        x_done = sem("x_done")
        copy_done = sem("copy_done")
        split_hi_done = sem("split_hi_done")
        split_done = sem("split_done")
        y_done = sem("y_done")
        y_free = sem("y_free")
        rot_in = [sem("rot_in0"), sem("rot_in1")]
        product_done = sem("product_done")
        start_product_done = sem("start_product_done")
        rope_sum_done = sem("rope_sum_done")
        rope_hi_done = sem("rope_hi_done")
        rope_lo_done = sem("rope_lo_done")
        rcp_done = sem("rcp_done")
        stats_done = sem("stats_done")
        var_done = sem("var_done")
        std_done = sem("std_done")
        inv_done = sem("inv_done")
        ln_done = sem("ln_done")
        sq_done = sem("sq_done")
        nx_done = sem("nx_done")
        gu_done = sem("gu_done")
        silu_done = sem("silu_done")
        prod_done = sem("prod_done")
        act_hi_done = sem("act_hi_done")
        act_lo_done = sem("act_lo_done")
        out_ready, last_ready = sem("out_ready"), sem("last_ready")
        shift_done = sem("shift_done")
        out_done = sem("out_done")
        warm_done = sem("warm_done")
        eps_done = sem("eps_done")

        block = ctx.enter_context(nc.Block())

        @block.sync
        def _(sp):
            sp.dma_start(wq_raw[:], wq_v[:, :, 0:HD]).then_inc(wq_in, 16)
            for arrived, (half, begin, end) in zip(x_t_in, X_PARTS):
                if (half, begin) == (1, 0):
                    sp.dma_start(wkv_raw[:], wk_v[:, :, 0:HD]).then_inc(wkv_in, 16)
                cols = slice(half * HALF, (half + 1) * HALF)
                sp.dma_start(xT_raw[:, begin:end, cols], x_t_v[:, begin:end, cols]).then_inc(arrived, 16)
            sp.dma_start(cos_sb[:], cos_t).then_inc(cos_in, 16)
            sp.dma_start(sin_sb[:], sin_t).then_inc(sin_in, 16)
            sp.wait_ge(wkv_done, 1)
            sp.dma_start(wkv_raw[:], wv_v[:, :, 0:HD]).then_inc(wkv_in, 16)

            def load_wq(h):
                sp.wait_ge(wq_done, h)
                sp.dma_start(wq_raw[:], wq_v[:, :, bass.ds(h * HD, HD)]).then_inc(wq_in, 16)

            def load_wo(h):
                sp.wait_ge(wo_done, h)
                sp.dma_start(wo_raw[:], wo[bass.ds(h * HD, HD), :]).then_inc(wo_in, 16)

            n = Tally()

            def rotate():
                r, h = n.n["rope"] % 2, HD // 2
                n.add("copy")
                sp.wait_ge(copy_done, n["copy"])
                sp.dma_start(rope_s[0:h, r], qk_raw[h:P, r]).then_inc(rot_in[r], 16)
                sp.dma_start(rope_s[h:P, r], qk_raw[0:h, r]).then_inc(rot_in[r], 16)
                n.add("rope")

            def step(j, i, last=False):
                for kind, _, _ in finished(j, i, last):
                    if kind in "qk":
                        rotate()
                    n.add("copy", kind == "v")

            for u, (kind, _) in enumerate(START):
                if kind in "qk":
                    rotate()
                n.add("copy", kind == "v")
                if u == 0:
                    load_wq(1)
                if u == 1:
                    sp.dma_start(wo_raw[:], wo[0:HD, :]).then_inc(wo_in, 16)
            load_wq(2)
            sp.wait_ge(xt_lo_done, 2 * NC)
            sp.dma_start(y[:], x_v).then_inc(x_in, 16)
            for j, i in FIRST_HEAD:
                step(j, i)
                if i == 1:
                    with nc.allow_non_contiguous_dma(reason="512 words, once"):
                        sp.dma_start(ln_w_sb[:], ln_w_v).then_inc(ln_w_in, 16)
                    sp.dma_start(gate_raw[:], gate_v[:, :, 0:2 * P]).then_inc(gate_in, 16)
                    sp.dma_start(up_raw[:], up_v[:, :, 0:2 * P]).then_inc(up_in, 16)
            with sp.Fori(0, GROUPS - 1) as g:
                n.enter(g)
                for j, i in LOOP_STEPS:
                    if i == 0:
                        if j == 1:
                            sp.wait_ge(wkv_done, g * 2 + 2)
                            sp.dma_start(wkv_raw[:], wk_v[:, :, bass.ds(g * HD + HD, HD)]).then_inc(wkv_in, 16)
                        load_wo(g * REP + j)
                        load_wq(g * REP + (j + 2))
                    if (j, i) == (2, 0):
                        sp.wait_ge(wkv_done, g * 2 + 3)
                        sp.dma_start(wkv_raw[:], wv_v[:, :, bass.ds(g * HD + HD, HD)]).then_inc(wkv_in, 16)
                    step(j, i)
            n.leave(GROUPS - 1)
            for j, i in LAST_STEPS:
                if i == 0:
                    load_wo((GROUPS - 1) * REP + j)
                    if j + 2 < REP:
                        load_wq((GROUPS - 1) * REP + j + 2)
                step(j, i, last=True)

            def load_gate_up(p):
                sp.wait_ge(fw_lo_done, p * 3 - 1)
                cols = bass.ds(p * 2 * P, 2 * P)
                sp.dma_start(gate_raw[:], gate_v[:, :, cols]).then_inc(gate_in, 16)
                sp.dma_start(up_raw[:], up_v[:, :, cols]).then_inc(up_in, 16)

            def load_down(p):
                sp.dma_start(down_raw, down_v[:, bass.ds(p * 2, 2), :]).then_inc(down_in, 16)

            sp.wait_ge(tp_done, HEADS * 12)
            load_down(0)
            load_gate_up(1)
            with sp.Fori(1, PAIRS - 1) as p:
                sp.wait_ge(fw_lo_done, p * 3)
                load_down(p)
                load_gate_up(p + 1)
            sp.wait_ge(fw_lo_done, (PAIRS - 1) * 3)
            load_down(PAIRS - 1)

            for t in range(NT):
                sp.wait_ge(*((out_ready, t + 1) if t < SCALAR_TILES else (last_ready, t + 1 - SCALAR_TILES)))
                sp.dma_start(out_v[:, t, :], y[:, t, :]).then_inc(out_done, 16)
            sp.wait_ge(out_done, 16 * NT)

        @block.gpsimd
        def _(pool):
            n = Tally()

            nc.gpsimd.memset(ident[:], 0.0).then_inc(const_done, 1)
            nc.gpsimd.memset(mask[:], 0.0).then_inc(const_done, 1)
            nc.gpsimd.memset(zero[:], 0.0).then_inc(const_done, 1)
            pool.wait_ge(const_done, 3)
            nc.gpsimd.affine_select(out=ident[:], in_=ident[:], compare_op=ALU.not_equal, fill=1.0, base=0,
                                    pattern=[[-1, P]], channel_multiplier=1).then_inc(const_done, 1)
            nc.gpsimd.affine_select(out=mask[:], in_=mask[:], compare_op=ALU.is_ge, fill=MASKED, base=0,
                                    pattern=[[-1, P]], channel_multiplier=1).then_inc(const_done, 1)

            def split(kind, raw, hi, lo, arrived, done):
                pool.wait_ge(arrived, n[kind] * 16 + 16)
                nc.gpsimd.tensor_tensor(hi, raw, zero[:, 0:1].to_broadcast([P, NC * HD]), ALU.add).then_inc(w_hi_done, 1)
                pool.wait_ge(w_hi_done, n["wq"] + n["wo"] + n["wkv"] + 1)
                nc.gpsimd.tensor_tensor(lo, raw, hi.bitcast(F32), ALU.subtract).then_inc(done, 1)
                n.add(kind)

            def flat(a):
                return a[:].rearrange("p a b -> p (a b)")

            def split_wq():
                split("wq", flat(wq_raw), flat(wq_hi), flat(wq_lo), wq_in, wq_done)

            def split_wkv(first=False):
                hi, lo = (wo_hi[:, 1], wo_lo[:, 1]) if first else (flat(wkv_hi), flat(wkv_lo))
                split("wkv", flat(wkv_raw), hi, lo, wkv_in, wkv_done)

            def split_wo():
                slot = n.n["wo"] % 2
                split("wo", wo_raw[:], wo_hi[:, slot], wo_lo[:, slot], wo_in, wo_done)

            def rope_cos(half):
                r, cols = n.n["rope"] % 2, slice(half * HALF, (half + 1) * HALF)
                pool.wait_ge(copy_done, n["copy"] + 1)
                if n.n["rope"] >= 2:
                    pool.wait_ge(rope_lo_done, n["rope"] - 1)
                nc.gpsimd.tensor_tensor(rope_c[:, r], qk_raw[:, r], cos_sb[:, cols], ALU.mult).then_inc(product_done, 1)
                n.add("rope")
                n.add("product")
                n.add(f"rot{r}")

            def rope_sin(half, ago):
                r, cols = (n.n["rope"] - 1 - ago) % 2, slice(half * HALF, (half + 1) * HALF)
                pool.wait_ge(rot_in[r], n[f"rot{r}"] * 32)
                nc.gpsimd.tensor_tensor(rope_s[:, r], rope_s[:, r], sin_sb[:, cols], ALU.mult).then_inc(product_done, 1)
                n.add("product")

            def rope_add(ago=0):
                r = (n.n["rope"] - 1 - ago) % 2
                pool.wait_ge(product_done, n["product"])
                nc.gpsimd.tensor_tensor(rope_c[:, r], rope_c[:, r], rope_s[:, r], ALU.add).then_inc(rope_sum_done, 1)

            def rope_low(hi, lo, ago=0):
                r = (n.n["rope"] - 1 - ago) % 2
                pool.wait_ge(rope_hi_done, n["rope"] - ago)
                nc.gpsimd.tensor_tensor(lo, rope_c[:, r], hi.bitcast(F32), ALU.subtract).then_inc(rope_lo_done, 1)

            def half_of(a, slot, half):
                return a[:, slot, half * HALF:(half + 1) * HALF]

            def k_half(a, slot, half):
                return a[:, bass.ds(slot, 1), half * HALF:(half + 1) * HALF].rearrange("p a b -> p (a b)")

            def qk_halves(kind, half, head, k_slot):
                if kind == "q":
                    return [half_of(a, head % 2, half) for a in (Q_hi, Q_lo)]
                return [k_half(a, k_slot, half) for a in (K_hi, K_lo)]

            def step(j, i, k_slot, last=False):
                if i == 1 and not last and j in (1, 3):
                    pool.wait_ge(x_done, n["x"])
                    split_wkv()
                for _, half, _, later, _ in ropes_due("sum", j, i, last):
                    rope_sin(half, later)
                    rope_add(later)
                for kind, half, head, later, _ in ropes_due("low", j, i, last):
                    rope_low(*qk_halves(kind, half, head, k_slot), later)
                if i == 3 and not (last and j >= REP - 2):
                    pool.wait_ge(x_done, n["x"])
                    split_wq()
                if i == 5:
                    if j > 0:
                        pool.wait_ge(y_done, n["y"])
                    split_wo()
                for kind, half, head in finished(j, i, last):
                    if kind in "qk":
                        rope_cos(half)
                    n.add("copy", kind in "qkv")
                    n.add("x")
                n.add("y", j > 0)

            pool.wait_ge(wq_done, 1)
            n.add("wq")
            split_wkv()
            split_wkv(first=True)
            pool.wait_ge(x_done, 3)
            split_wq()
            pool.wait_ge(cos_in, 16)
            pool.wait_ge(sin_in, 16)
            pool.wait_ge(rope_lo_done, 4)
            n.add("copy", len(START))
            n.add("x", len(START))
            n.add("rope", 4)
            n.add("rot0", 2)
            n.add("rot1", 2)
            for j, i in FIRST_HEAD:
                step(j, i, 0)
            with pool.Fori(0, GROUPS - 1) as g:
                n.enter(g)
                k_slot = pool.snap((g + 1) % 2)
                for j, i in LOOP_STEPS:
                    step(j, i, k_slot)
            n.leave(GROUPS - 1)
            for j, i in LAST_STEPS:
                step(j, i, 0, last=True)

            def act_low(u, unit_no):
                pool.wait_ge(act_hi_done, unit_no)
                half, i2 = divmod(u, 2)
                cols = slice(half * HALF, (half + 1) * HALF)
                nc.gpsimd.tensor_tensor(act[1][:, i2, cols], rope_s[:, u % 2], act[0][:, i2, cols].bitcast(F32),
                                        ALU.subtract).then_inc(act_lo_done, 1)

            def weight_low(number, raw, w):
                pool.wait_ge(fw_hi_done, number + 1)
                nc.gpsimd.tensor_tensor(w[1], raw, w[0].bitcast(F32), ALU.subtract).then_inc(fw_lo_done, 1)

            def pair(p, last=False):
                for u in range(4):
                    act_low(u, p * 4 + (u + 1))
                    if u == 0:
                        weight_low(p * 3 + 2, down_raw, dT)
                if not last:
                    weight_low(p * 3 + 3, gate_raw[:], gT)
                    weight_low(p * 3 + 4, up_raw[:], uT)

            weight_low(0, gate_raw[:], gT)
            weight_low(1, up_raw[:], uT)
            with pool.Fori(0, PAIRS - 1) as p:
                pair(p)
            pair(PAIRS - 1, last=True)

        @block.scalar
        def _(act_e):
            n = Tally()

            def exponent(j, i):
                slot, at = n.n["tile"] % 2, n.n["tile"] % 4
                act_e.wait_ge(max_done, n["tile"] + 1)
                width = P * (i + 1)
                src, dst = S[:, slot, 0:width], probs[:, slot, 0:width]
                if width > 512:
                    src = S[:, slot].rearrange("p (a b) -> p a b", a=2)[:, :, 0:width // 2]
                    dst = dst.rearrange("p (a b) -> p a b", a=2)
                nc.scalar.activation(dst, src, ACT.Exp, bias=neg_max[:, at:at + 1],
                                     accum_out=row_sum[:, j % 2, i:i + 1]).then_inc(exp_done, 1)
                n.add("tile")

            def tp_high(i):
                for u in range(tp_banks(i)):
                    act_e.wait_ge(tp_done, n["pt"] + 1)
                    dst, src = pt_views(PT_hi, i, u, n.n["pt"] % 2)
                    nc.scalar.activation(dst, src, ACT.Copy).then_inc(tp_hi_done, 1)
                    n.add("pt")

            def rope_high(hi, ago=0):
                act_e.wait_ge(rope_sum_done, n["rope"] - ago)
                nc.scalar.activation(hi, rope_c[:, (n.n["rope"] - 1 - ago) % 2], ACT.Copy).then_inc(rope_hi_done, 1)

            def copy_out(kind, half, bank=0):
                act_e.wait_ge(x_done, n["x"] + 1)
                dst = qk_raw[:, n.n["rope"] % 2] if kind in "qk" else V_stage[:, half * HALF:(half + 1) * HALF]
                if kind in "qk" and n.n["rope"] >= 2:
                    act_e.wait_ge(rope_sum_done, n["rope"] - 1)
                nc.scalar.activation(dst, ACC[:, bank], ACT.Copy).then_inc(copy_done, 1)
                n.add("rope", kind in "qk")
                n.add("x")

            def split_high(kind, half):
                act_e.wait_ge(x_done, n["x"] + 1)
                dst = O_hi[:, half * HALF:(half + 1) * HALF] if kind == "pv" else \
                    V_hi[:, half * HT:(half + 1) * HT, :].rearrange("p a b -> p (a b)")
                nc.scalar.activation(dst, ACC[:, 0], ACT.Copy).then_inc(split_hi_done, 1)
                n.add("x")

            def step(j, i, k_slot, last=False):
                for kind, half, head in finished(j, i, last):
                    if kind in "qkv":
                        copy_out(kind, half)
                    else:
                        split_high(kind, half)
                tp_high(i)
                if not (last and (j, i) == LAST_STEPS[-1]):
                    exponent(j + (i + 1) // NT, (i + 1) % NT)
                for kind, half, head, _, later in ropes_due("high", j, i, last):
                    cols = slice(half * HALF, (half + 1) * HALF)
                    hi = Q_hi[:, head % 2, cols] if kind == "q" else \
                        K_hi[:, bass.ds(k_slot, 1), cols].rearrange("p a b -> p (a b)")
                    rope_high(hi, later)

            def xT_high(half, count, banks, scale=False):
                for c in range(NC):
                    act_e.wait_ge(xt_done, count + c + 1)
                    nc.scalar.activation(xT_hi[:, c, half * HALF:(half + 1) * HALF], banks[c], ACT.Copy,
                                         scale=ln_w_sb[:, c:c + 1] if scale else 1.0).then_inc(xt_hi_done, 1)

            act_e.wait_ge(wq_in, 16)
            nc.scalar.activation(wq_hi[:], wq_raw[:], ACT.Copy).then_inc(w_hi_done, 1)
            for arrived, (half, begin, end) in zip(x_t_in, X_PARTS):
                act_e.wait_ge(arrived, 16)
                for c in range(begin, end):
                    cols = slice(half * HALF, (half + 1) * HALF)
                    nc.scalar.activation(xT_hi[:, c, cols], xT_raw[:, c, cols], ACT.Copy).then_inc(xt_hi_done, 1)

            def start_high(u, ago):
                kind, half = START[u]
                rope_high((Q_hi if kind == "q" else K_hi)[:, 0, half * HALF:(half + 1) * HALF], ago)

            for u, (kind, half) in enumerate(START):
                if u in (2, 3, 4):
                    start_high(u - 2, 1)
                copy_out(kind, half, u % 2)
            exponent(0, 0)
            start_high(3, 0)
            for j, i in FIRST_HEAD:
                step(j, i, 0)
            with act_e.Fori(0, GROUPS - 1) as g:
                n.enter(g)
                k_slot = act_e.snap((g + 1) % 2)
                for j, i in LOOP_STEPS:
                    step(j, i, k_slot)
            n.leave(GROUPS - 1)
            for j, i in LAST_STEPS:
                step(j, i, 0, last=True)

            def deviation(cols, squares, eps, scale):
                nc.scalar.activation(spread[:, cols], squares, ACT.Sqrt, bias=eps[:], scale=scale).then_inc(std_done, 1)

            def layer_deviation(half):
                act_e.wait_ge(var_done, (half + 1) * HT)
                cols = slice(half * HT, (half + 1) * HT)
                deviation(cols, mean_var[:, cols, 1], eps_ln, 1.0)

            def rms_deviation(half):
                for t in range(half * HT, (half + 1) * HT):
                    act_e.wait_ge(ln_done, t + 1)
                    if t >= 2:
                        act_e.wait_ge(sq_done, t - 1)
                    nc.scalar.activation(V_stage[:, t % 2 * HID:(t % 2 + 1) * HID], y[:, t, :], ACT.Square,
                                         accum_out=sum_sq[:, t:t + 1]).then_inc(sq_done, 1)
                act_e.wait_ge(sq_done, (half + 1) * HT)
                cols = slice(half * HT, (half + 1) * HT)
                deviation(cols, sum_sq[:, cols], eps_rms, 1.0 / HID)

            def weight_high(p, which):
                raw, w = ((gate_raw[:], gT), (up_raw[:], uT), (down_raw, dT))[which]
                act_e.wait_ge((gate_in, up_in, down_in)[which], p * 16 + 16)
                nc.scalar.activation(w[0], raw, ACT.Copy).then_inc(fw_hi_done, 1)

            def silu(p, u):
                act_e.wait_ge(gu_done, p * 4 + (u + 1))
                nc.scalar.activation(rope_c[:, u % 2], S[:, u % 2, 0:HALF], ACT.Silu).then_inc(silu_done, 1)

            def act_high(p, u):
                half, i2 = divmod(u, 2)
                act_e.wait_ge(prod_done, p * 4 + (u + 1))
                cols = slice(half * HALF, (half + 1) * HALF)
                nc.scalar.activation(act[0][:, i2, cols], rope_s[:, u % 2], ACT.Copy).then_inc(act_hi_done, 1)

            def pair(p, first=False, last=False):
                for u in range(4):
                    silu(p, u)
                    if first and u == 0:
                        xT_high(1, NC, xbank[1], scale=True)
                    act_high(p, u)
                    if u == 0:
                        if not first:
                            act_e.wait_ge(y_done, p * NT + y_base)
                        weight_high(p, 2)
                if not last:
                    weight_high(p + 1, 0)
                    weight_high(p + 1, 1)

            y_base = HEADS * NT
            act_e.wait_ge(eps_done, 1)
            nc.scalar.activation(table_scratch[:], eps_ln[:], ACT.Sqrt)
            layer_deviation(0)
            split_high("pv", 1)
            rms_deviation(0)
            weight_high(0, 0)
            weight_high(0, 1)
            act_e.wait_ge(ln_w_in, 16)
            xT_high(0, 0, xbank[0], scale=True)
            layer_deviation(1)
            rms_deviation(1)
            pair(0, first=True)
            with act_e.Fori(1, PAIRS - 1) as p:
                pair(p)
            pair(PAIRS - 1, last=True)

            def normalise(t):
                act_e.wait_ge(shift_done, t + 1)
                nc.scalar.activation(y[:, t, :], y[:, t, :], ACT.Identity, bias=shift[:, t:t + 1],
                                     scale=inv_spread[:, t:t + 1]).then_inc(out_ready, 1)

            for t in range(NT):
                act_e.wait_ge(var_done, NT + t + 1)
                deviation(slice(t, t + 1), mean_var[:, t, 1:2], eps_ln, 1.0)
                if t >= 1:
                    normalise(t - 1)

        @block.vector
        def _(dve):
            n = Tally()

            def maximum(i):
                slot, at = n.n["tile"] % 2, n.n["tile"] % 4
                dve.wait_ge(score_done, n["tile"] + 1)
                width = P * (i + 1)
                src = S[:, slot, 0:width]
                if width > 512:
                    src = S[:, slot].rearrange("p (a b) -> p a b", a=2)[:, :, 0:width // 2]
                col, _, keys = score_chunks(i)[-1]
                diagonal = S[:, slot, col + keys - P:col + keys]
                nc.vector.tensor_tensor(diagonal, diagonal, mask[:], ALU.add).then_inc(mask_done, 1)
                dve.wait_ge(mask_done, n["tile"] + 1)
                if n.n["tile"] >= 4:
                    dve.wait_ge(exp_done, n["tile"] - 3)
                nc.vector.tensor_reduce(neg_max[:, at:at + 1], src, AX.XY if width > 512 else AX.X, ALU.max,
                                        negate=True).then_inc(max_done, 1)
                n.add("tile")

            def tp_low(i):
                for u in range(tp_banks(i)):
                    dve.wait_ge(tp_hi_done, n["pt"] + 1)
                    hi, src = pt_views(PT_hi, i, u, n.n["pt"] % 2)
                    lo, _ = pt_views(PT_lo, i, u, n.n["pt"] % 2)
                    nc.vector.tensor_tensor(lo, src, hi.bitcast(F32), ALU.subtract).then_inc(tp_lo_done, 1)
                    n.add("pt")

            def start_low(k):
                dve.wait_ge(rope_hi_done, k + 1)
                kind, half = START[k]
                hi, lo = [a[:, 0, half * HALF:(half + 1) * HALF] for a in ((Q_hi, Q_lo) if kind == "q" else (K_hi, K_lo))]
                nc.vector.tensor_tensor(lo, rope_c[:, k % 2], hi.bitcast(F32), ALU.subtract).then_inc(rope_lo_done, 1)

            def start_rope(k, meanwhile=None):
                half, r = START[k][1], k % 2
                cols = slice(half * HALF, (half + 1) * HALF)
                dve.wait_ge(copy_done, k + 1)
                if k >= 2:
                    dve.wait_ge(rope_lo_done, k - 1)
                nc.vector.tensor_tensor(rope_c[:, r], qk_raw[:, r], cos_sb[:, cols], ALU.mult).then_inc(start_product_done, 1)
                if k >= 1:
                    start_low(k - 1)
                if meanwhile:
                    meanwhile()
                dve.wait_ge(rot_in[r], (k // 2 + 1) * 32)
                nc.vector.tensor_tensor(rope_s[:, r], rope_s[:, r], sin_sb[:, cols], ALU.mult).then_inc(start_product_done, 1)
                dve.wait_ge(start_product_done, 2 * k + 2)
                nc.vector.tensor_tensor(rope_c[:, r], rope_c[:, r], rope_s[:, r], ALU.add).then_inc(rope_sum_done, 1)

            def split_low(kind, half, head):
                dve.wait_ge(split_hi_done, n["split"] + 1)
                hi, lo = [a[:, half * HALF:(half + 1) * HALF] for a in (O_hi, O_lo)] if kind == "pv" else \
                    [a[:, half * HT:(half + 1) * HT, :].rearrange("p a b -> p (a b)") for a in (V_hi, V_lo)]
                nc.vector.tensor_tensor(lo, ACC[:, 0], hi.bitcast(F32), ALU.subtract).then_inc(split_done, 1)
                n.add("split")
                if kind == "pv":
                    reciprocals(head, half)

            def reciprocals(head, half):
                rows = slice(half * HT, (half + 1) * HT)
                nc.vector.reciprocal(row_rcp[:, head % 2, rows], row_sum[:, head % 2, rows]).then_inc(rcp_done, 1)
                n.add("recip")

            def add_rows(t, head, tail=False):
                dve.wait_ge(y_done, n["y"] + 1)
                dve.wait_ge(rcp_done, n["recip"])
                nc.vector.scalar_tensor_tensor(out=y[:, t, :], in0=ACC[:, y_bank(t, tail)],
                                               scalar=row_rcp[:, head % 2, t:t + 1], in1=y[:, t, :],
                                               op0=ALU.mult, op1=ALU.add).then_inc(y_free, 1)
                n.add("y")

            def step(j, i, last=False):
                if not (last and (j, i) == LAST_STEPS[-1]):
                    maximum((i + 1) % NT)
                for kind, half, head in finished(j, i, last):
                    if kind in ("pv", "vt"):
                        split_low(kind, half, head)
                tp_low(i)
                if j > 0:
                    add_rows(i, j - 1)

            nc.vector.memset(eps_ln[:], LN_EPS).then_inc(eps_done, 1)
            dve.wait_ge(w_hi_done, 1)
            nc.vector.tensor_tensor(wq_lo[:], wq_raw[:], wq_hi[:].bitcast(F32), ALU.subtract).then_inc(wq_done, 1)
            for half in range(2):
                for c in range(NC):
                    dve.wait_ge(xt_hi_done, half * NC + c + 1)
                    cols = slice(half * HALF, (half + 1) * HALF)
                    nc.vector.tensor_tensor(xT_lo[:, c, cols], xT_raw[:, c, cols], xT_hi[:, c, cols].bitcast(F32),
                                            ALU.subtract).then_inc(xt_lo_done, 1)
            dve.wait_ge(cos_in, 16)
            dve.wait_ge(sin_in, 16)
            for k in range(3):
                start_rope(k)
            dve.wait_ge(const_done, 5)
            start_rope(3, meanwhile=lambda: maximum(0))
            start_low(3)
            dve.wait_ge(copy_done, len(START))
            nc.vector.memset(eps_rms[:], RMS_EPS).then_inc(y_free, 1)
            for j, i in FIRST_HEAD:
                step(j, i)
            dve.wait_ge(x_in, 16)
            with dve.Fori(0, GROUPS - 1) as g:
                n.enter(g)
                for j, i in LOOP_STEPS:
                    step(j, i)
            n.leave(GROUPS - 1)
            for j, i in LAST_STEPS:
                step(j, i, last=True)

            def product(p, u, first=False):
                dve.wait_ge(silu_done, p * 4 + (u + 1))
                if u >= 2 or not first:
                    dve.wait_ge(act_lo_done, p * 4 + (u - 1))
                nc.vector.tensor_tensor(rope_s[:, u % 2], S[:, u % 2, HALF:2 * HALF], rope_c[:, u % 2],
                                        ALU.mult).then_inc(prod_done, 1)

            def down_add(p, t):
                dve.wait_ge(y_done, p * NT + (y_base + t + 1))
                nc.vector.tensor_tensor(y[:, t, :], ACC[:, t % 2], y[:, t, :], ALU.add).then_inc(y_free, 1)

            def pair(p):
                for u in range(4):
                    product(p, u)
                for t in range(NT):
                    down_add(p, t)

            def statistics(t, rows_done):
                dve.wait_ge(y_free, rows_done + 1)
                nc.vector.bn_stats(stats[:, t, :], y[:, t, :]).then_inc(stats_done, 1)

            def aggregate(t):
                n.add("stats")
                dve.wait_ge(stats_done, n["stats"])
                nc.vector.bn_aggr(mean_var[:, t, :], stats[:, t, :]).then_inc(var_done, 1)

            def variances(ts, rows_done):
                for t in ts:
                    statistics(t, rows_done)
                for t in ts:
                    aggregate(t)

            def inverses(turn, cols):
                dve.wait_ge(std_done, turn)
                nc.vector.reciprocal(inv_spread[:, cols], spread[:, cols]).then_inc(inv_done, 1)
                dve.wait_ge(inv_done, turn)

            def layer_norm(t):
                return nc.vector.tensor_scalar(y[:, t, :], y[:, t, :], mean_var[:, t, 0:1], inv_spread[:, t:t + 1],
                                               ALU.subtract, ALU.mult)

            def rms_norm(t):
                nc.vector.tensor_scalar(nx[t], y[:, t, :], inv_spread[:, t:t + 1], None, ALU.mult).then_inc(nx_done, 1)

            def xT_low(half):
                for c in range(NC):
                    dve.wait_ge(xt_hi_done, (2 + half) * NC + c + 1)
                    cols = slice(half * HALF, (half + 1) * HALF)
                    nc.vector.scalar_tensor_tensor(out=xT_lo[:, c, cols], in0=xbank[half][c], scalar=ln_w_sb[:, c:c + 1],
                                                   in1=xT_hi[:, c, cols].bitcast(F32), op0=ALU.mult,
                                                   op1=ALU.subtract).then_inc(xt_lo_done, 1)

            tiles = [range(HT), range(HT, NT)]
            cols = [slice(0, HT), slice(HT, NT)]
            dve.wait_ge(ln_w_in, 16)
            for t in tiles[0]:
                add_rows(t, REP - 1, tail=True)
            variances(tiles[0], n["y"])
            inverses(1, cols[0])
            for t in tiles[0]:
                if t == 2:
                    split_low("pv", 1, REP - 1)
                layer_norm(t).then_inc(ln_done, 1)
            for t in (4, 5):
                add_rows(t, REP - 1, tail=True)
            inverses(2, cols[0])
            for t in tiles[0]:
                rms_norm(t)
            for t in (6, 7):
                add_rows(t, REP - 1, tail=True)
            y_base = n["y"]
            xT_low(0)
            variances(tiles[1], y_base)
            inverses(3, cols[1])
            for t in tiles[1]:
                layer_norm(t).then_inc(ln_done, 1)
            inverses(4, cols[1])
            for t in tiles[1]:
                rms_norm(t)
            product(0, 0, first=True)
            xT_low(1)

            for u in range(1, 4):
                product(0, u, first=True)
            for t in range(NT):
                down_add(0, t)
            with dve.Fori(1, PAIRS - 1) as p:
                pair(p)

            def inverse(t):
                dve.wait_ge(std_done, 5 + t)
                nc.vector.reciprocal(inv_spread[:, t:t + 1], spread[:, t:t + 1]).then_inc(inv_done, 1)

            def finish(t):
                dve.wait_ge(inv_done, 5 + t)
                if t < SCALAR_TILES:
                    nc.vector.scalar_tensor_tensor(out=shift[:, t:t + 1], in0=mean_var[:, t, 0:1], scalar=-1.0,
                                                   in1=inv_spread[:, t:t + 1], op0=ALU.mult, op1=ALU.mult).then_inc(shift_done, 1)
                else:
                    layer_norm(t).then_inc(last_ready, 1)

            for u in range(3):
                product(PAIRS - 1, u)
            early = range(EARLY_TILES)
            for t in range(NT):
                if t == EARLY_TILES:
                    product(PAIRS - 1, 3)
                down_add(PAIRS - 1, t)
                if t > EARLY_TILES:
                    for done in early if t == EARLY_TILES + 1 else [t - 2]:
                        finish(done)
                if t > 0:
                    aggregate(t - 1)
                statistics(t, y_base + (PAIRS - 1) * NT + t + 1)
                if t >= EARLY_TILES:
                    for done in early if t == EARLY_TILES else [t - 1]:
                        inverse(done)
            aggregate(NT - 1)
            finish(NT - 2)
            inverse(NT - 1)
            finish(NT - 1)

        @block.tensor
        def _(pe):
            n = Tally()

            def product(dst, a, b, start, stop):
                nc.tensor.matmul(dst, a[0], b[0], start=start, stop=False)
                nc.tensor.matmul(dst, a[0], b[1], start=False, stop=False)
                return nc.tensor.matmul(dst, a[1], b[0], start=False, stop=stop)

            def scores(j, i, k_slot):
                slot = n.n["tile"] % 2
                if i % HT == 0:
                    pe.wait_ge(rope_lo_done, n.marked(("q", i // HT, j % 2)))
                if n.n["tile"] >= 2:
                    pe.wait_ge(exp_done, n["tile"] - 1)
                q = [a[:, j % 2, i * P:(i + 1) * P] for a in (Q_hi, Q_lo)]
                for col, key, width in score_chunks(i):
                    dst = S[:, slot, col:col + width]
                    k = [a[:, bass.ds(k_slot, 1), key:key + width].rearrange("p a b -> p (a b)") for a in (K_hi, K_lo)]
                    nc.tensor.matmul(dst, q[0], k[0], start=True, stop=False)
                    nc.tensor.matmul(dst, q[0], k[1], start=False, stop=False)
                    last = nc.tensor.matmul(dst, q[1], k[0], start=False, stop=True)
                last.then_inc(score_done, 1)
                n.add("tile")

            def transposes(i, tile):
                pe.wait_ge(exp_done, n.at("tile", tile + 1))
                for u in range(tp_banks(i)):
                    bank = n.n["pt"] % 2
                    if n.n["pt"] >= 2:
                        pe.wait_ge(tp_lo_done, n["pt"] - 1)
                    for b in range(4 * u, min(4 * u + 4, i + 1)):
                        last = nc.tensor.transpose(TP[:, bank, (b % 4) * P:(b % 4 + 1) * P],
                                                   probs[:, tile % 2, b * P:(b + 1) * P], ident[:])
                    last.then_inc(tp_done, 1)
                    n.add("pt")
                n.mark(("pt", i), "pt")

            def other(kind, half, head, begin, end, bank=0, start=False):
                acc, count = ACC[:, bank], products(kind, half)
                if begin == 0 and ("bank", bank) in n.marks:
                    pe.wait_ge(copy_done if n.marks["bank", bank][0] == "copy" else split_done, n.marked(("bank", bank)))
                if begin == 0 and kind in "qkv":
                    if kind == "q":
                        pe.wait_ge(wq_done, n["wq"] + 1)
                    else:
                        pe.wait_ge(wkv_done, n["wkv"] + 1)
                if begin == 0 and kind == "pv":
                    pe.wait_ge(tp_lo_done, n.marked(("pt", HT * (half + 1) - 1)))
                for k in range(begin, end):
                    if start and kind == "q":
                        pe.wait_ge(xt_lo_done, half * NC + k + 1)
                    if kind in "qkv":
                        w = (wq_hi, wq_lo) if kind == "q" else (wkv_hi, wkv_lo)
                        if start and kind == "v":
                            w = [a[:, 1].rearrange("p (c n) -> p c n", n=HD) for a in (wo_hi, wo_lo)]
                        cols = slice(half * HALF, (half + 1) * HALF)
                        last = product(acc, [a[:, k, :] for a in w], [a[:, k, cols] for a in (xT_hi, xT_lo)],
                                       k == 0, k == count - 1)
                    if kind == "vt":
                        key = (half * HT + k) * P
                        last = nc.tensor.transpose(acc[:, k * P:(k + 1) * P], V_stage[:, key:key + P], ident[:])
                    if kind == "pv":
                        skip = max(0, k - HT * half) * P
                        row = HT * half + k
                        last = product(acc[:, skip:HALF], [v[:, k, :] for v in (V_hi, V_lo)],
                                       [p[:, row, skip:HALF] for p in (PT_hi, PT_lo)], k == 0, k == count - 1)
                if end < count:
                    return
                last.then_inc(x_done, 1)
                released = "copy" if kind in "qkv" else "split"
                n.add(released)
                n.mark(("bank", bank), released)
                if kind == "pv":
                    n.mark((kind, half), released)
                if kind in "qk":
                    n.add("rope")
                    n.mark((kind, half, head % 2), "rope")
                if half == 1 and kind in "qkv":
                    n.add("wq" if kind == "q" else "wkv")

            def rows(t, tail=False):
                if t % HT == 0:
                    pe.wait_ge(split_done, n.marked(("pv", t // HT)))
                pe.wait_ge(wo_done, n["wo"] + 1)
                bank = y_bank(t, tail)
                if not (tail and t in (0, HT + 1)):
                    pe.wait_ge(y_free, n["y"] + (0 if tail and t != HT else 1))
                cols, slot = slice(t * P, (t + 1) * P), n.n["wo"] % 2
                o, w = (O_hi[:, cols], O_lo[:, cols]), (wo_hi[:, slot], wo_lo[:, slot])
                product(ACC[:, bank], o, w, True, True).then_inc(y_done, 1)
                n.add("y")
                n.add("wo", t == NT - 1)

            def step(j, i, slots, last=False):
                tile = n.n["tile"] - 1
                if not (last and (j, i) == LAST_STEPS[-1]):
                    following = j + (i + 1) // NT
                    scores(following, (i + 1) % NT, slots[following // REP])
                for part in extras(j, i, last):
                    other(*part)
                transposes(i, tile)
                if j > 0:
                    rows(i)

            def transpose_rows(half):
                for t in range(half * HT, (half + 1) * HT):
                    pe.wait_ge(nx_done, t + 1)
                    for c in range(NC):
                        last = nc.tensor.transpose(xbank[half][c][:, t % HT * P:(t % HT + 1) * P],
                                                   nx[t][:, c * P:(c + 1) * P], ident[:])
                        if t % HT == HT - 1:
                            last.then_inc(xt_done, 1)

            pe.wait_ge(const_done, 5)
            for _ in range(WARM_UP):
                nc.tensor.matmul(TP[:, 1, 0:P], ident[:], ident[:], start=True, stop=True).then_inc(warm_done, 1)
            pe.wait_ge(warm_done, WARM_UP)
            for u, (kind, half) in enumerate(START):
                other(kind, half, 0, 0, NC, bank=u % 2, start=True)
                if kind == "k":
                    n.mark(("q", half, 0), "rope")
            scores(0, 0, 0)
            for j, i in FIRST_HEAD:
                step(j, i, (0, 0))
            with pe.Fori(0, GROUPS - 1) as g:
                n.enter(g)
                slots = (pe.snap(g % 2), pe.snap((g + 1) % 2))
                for j, i in LOOP_STEPS:
                    step(j, i, slots)
            n.leave(GROUPS - 1)
            for j, i in LAST_STEPS:
                step(j, i, ((GROUPS - 1) % 2, 0), last=True)

            def gate_up(p, u, first=False):
                half, i2 = divmod(u, 2)
                if u >= 2 or not first:
                    pe.wait_ge(prod_done, p * 4 + (u - 1))
                cols, rows = slice(half * HALF, (half + 1) * HALF), slice(i2 * P, (i2 + 1) * P)
                for bank, w in enumerate((gT, uT)):
                    if u == 0:
                        pe.wait_ge(fw_lo_done, p * 3 + (1 + bank))
                    for c in range(NC):
                        if first and (u, bank, c) == (1, 1, NC // 2):
                            pe.wait_ge(y_free, y_base + 1)
                            transpose_rows(1)
                        if first and u % 2 == 0 and bank == 0:
                            pe.wait_ge(xt_lo_done, (2 + half) * NC + c + 1)
                        last = product(S[:, u % 2, bank * HALF:(bank + 1) * HALF], [a[:, c, rows] for a in w],
                                       [a[:, c, cols] for a in (xT_hi, xT_lo)], c == 0, c == NC - 1)
                last.then_inc(gu_done, 1)

            def down(p, t):
                if t % HT == 0:
                    pe.wait_ge(act_lo_done, p * 4 + (2 + t // HT * 2))
                pe.wait_ge(y_free, p * NT + (y_base + t))
                cols = slice(t * P, (t + 1) * P)
                for i2 in range(2):
                    last = product(ACC[:, t % 2], [a[:, i2, cols] for a in act], [a[:, i2, :] for a in dT],
                                   i2 == 0, i2 == 1)
                last.then_inc(y_done, 1)

            def pair(p):
                for u in range(4):
                    gate_up(p, u)
                downs(p)

            def downs(p, tiles=range(NT)):
                if 0 in tiles:
                    pe.wait_ge(fw_lo_done, p * 3 + 3)
                for t in tiles:
                    down(p, t)

            for t in range(HT):
                rows(t, tail=True)
            pe.wait_ge(y_free, n["y"])
            other("pv", 1, REP - 1, 0, NT)
            for t in range(HT, NT):
                rows(t, tail=True)
            y_base = n["y"]
            transpose_rows(0)
            gate_up(0, 0, first=True)
            gate_up(0, 1, first=True)
            gate_up(0, 2, first=True)
            gate_up(0, 3, first=True)
            downs(0)
            with pe.Fori(1, PAIRS - 1) as p:
                pair(p)
            for u in range(3):
                gate_up(PAIRS - 1, u)
            downs(PAIRS - 1, range(EARLY_TILES))
            gate_up(PAIRS - 1, 3)
            downs(PAIRS - 1, range(EARLY_TILES, NT))


def rope_tables():
    import numpy as np
    theta, factor, hi_ff, lo_ff, orig_max = 500000.0, 8.0, 4.0, 1.0, 1024
    inv = 1.0 / theta ** (np.arange(0, HD, 2, dtype=np.float64) / HD)
    wavelen = 2.0 * np.pi / inv
    low_wl, high_wl = orig_max / lo_ff, orig_max / hi_ff
    smooth = (orig_max / wavelen - lo_ff) / (hi_ff - lo_ff)
    scaled = np.where(wavelen > low_wl, inv / factor, inv)
    mid = (wavelen <= low_wl) & (wavelen >= high_wl)
    scaled = np.where(mid, (1 - smooth) * inv / factor + smooth * inv, scaled).astype(np.float32)
    freqs = np.arange(T, dtype=np.float32)[None, :] * scaled[:, None]
    scale = float(HD) ** -0.25
    cos = np.cos(freqs).astype(np.float64) * scale
    sin = np.sin(freqs).astype(np.float64) * scale
    return (np.concatenate([cos, cos]).astype(np.float32), np.concatenate([-sin, sin]).astype(np.float32))


_INS = ['L0_attn_x', 'L0_attn_wq', 'L0_attn_wk', 'L0_attn_wv', 'L0_attn_wo',
        'L0_ffn_ln_w', 'L0_ffn_gate_w', 'L0_ffn_up_w', 'L0_ffn_down_w']


def kernel(**inputs):
    import numpy as np
    import concourse.bacc as bacc
    from concourse.bass_utils import run_bass_kernel_spmd

    nc = bacc.Bacc("TRN2", target_bir_lowering=False, num_devices=1)
    arrays, args = {}, []
    for name in _INS:
        if "ffn" not in name or name.endswith("ln_w"):
            arrays[f"in_{name}_dram"] = np.ascontiguousarray(inputs[name])
        else:
            arrays[f"in_{name}_t_dram"] = np.ascontiguousarray(np.asarray(inputs[name]).T)
        if name == "L0_attn_x":
            arrays[f"in_{name}_t_dram"] = np.ascontiguousarray(np.asarray(inputs[name])[0].T)
    for name, table in zip(("cos", "sin"), rope_tables()):
        arrays[f"in_{name}_dram"] = table
    for name, a in arrays.items():
        args.append(nc.dram_tensor(name, a.shape, mybir.dt.from_np(a.dtype), kind="ExternalInput").ap())
    args.append(nc.dram_tensor("out_0_dram", (1, T, HID), F32, kind="ExternalOutput").ap())
    layer_kernel(nc, *args)
    r = run_bass_kernel_spmd(nc, [arrays], core_ids=[0])
    return r.results[0]["out_0_dram"]
```
